# Optimizing a Trainium2 kernel written in Bass

```python
import numpy as np
import jax
import jax.numpy as jnp

def _softmax(x, axis=-1):
    return jax.nn.softmax(x, axis=axis)

def _gelu(x):
    return jax.nn.gelu(x, approximate=True)

def _silu(x):
    return jax.nn.silu(x)

def _sigmoid(x):
    return jax.nn.sigmoid(x)

def _layernorm(x, axis=-1, eps=1e-05):
    m = jnp.mean(x, axis=axis, keepdims=True)
    v = jnp.var(x, axis=axis, keepdims=True)
    return (x - m) / jnp.sqrt(v + eps)

def _scatter_add(tgt, idx, src, axis=0):
    return tgt.at[idx].add(src)

def _segment_sum(src, seg, n):
    return jax.ops.segment_sum(src, seg, n)
kernel_name = 'mk_recurrent_d1_jaxref_r4_087aae'

def setup_inputs(seed: int=0):
    np.random.seed(seed)
    _w = jnp.asarray

    def _L0_attn_setup():
        import jax, jax.numpy as jnp
        import numpy as np
        import math
        EPS_LN = 1e-05
        SCALE = 16.0

        def layer_norm(x, g):
            mean = jnp.mean(x, axis=-1, keepdims=True)
            var = jnp.var(x, axis=-1, keepdims=True)
            return (x - mean) * jax.lax.rsqrt(var + EPS_LN) * g

        def l2norm(t):
            n = jnp.linalg.norm(t, axis=-1, keepdims=True)
            return t / jnp.maximum(n, 1e-12)
        key = jax.random.key(seed)
        ks = jax.random.split(key, 4)
        b, n, dim, h, dh = (4, 512, 256, 8, 64)
        inner = h * dh
        x = jax.random.normal(ks[0], (b, n, dim), dtype=jnp.float32)
        Wq = jax.random.normal(ks[1], (dim, inner), dtype=jnp.float32) * dim ** (-0.5)
        Wkv = jax.random.normal(ks[2], (dim, 2 * dh), dtype=jnp.float32) * dim ** (-0.5)
        Wout = jax.random.normal(ks[3], (inner, dim), dtype=jnp.float32) * inner ** (-0.5)
        norm_g = jnp.ones((dim,), dtype=jnp.float32)
        out_norm_g = jnp.ones((dim,), dtype=jnp.float32)
        return {'x': x, 'norm_g': norm_g, 'Wq': Wq, 'Wkv': Wkv, 'Wout': Wout, 'out_norm_g': out_norm_g}
    _L0_attn_in = _L0_attn_setup()

    def _L0_ffn_setup():
        import jax, jax.numpy as jnp
        import numpy as np
        TOP_K = 2
        CAP_FACTOR = 1.25

        def _gelu(x):
            return 0.5 * x * (1.0 + jnp.tanh(jnp.sqrt(2.0 / jnp.pi) * (x + 0.044715 * x ** 3)))
        key = jax.random.key(seed)
        ks = jax.random.split(key, 6)
        B, S, D, F, E = (4, 512, 256, 1024, 8)
        return {'hidden_states': jax.random.normal(ks[0], (B, S, D), dtype=jnp.float32), 'wr': jax.random.normal(ks[1], (E, D), dtype=jnp.float32) * 0.02, 'w1': jax.random.normal(ks[2], (E, D, F), dtype=jnp.float32) * 0.02, 'b1': jnp.zeros((E, F), dtype=jnp.float32), 'w2': jax.random.normal(ks[3], (E, F, D), dtype=jnp.float32) * 0.02, 'b2': jnp.zeros((E, D), dtype=jnp.float32)}
    _L0_ffn_in = _L0_ffn_setup()
    _d = {'L0_attn_x': _L0_attn_in['x'], 'L0_attn_norm_g': _L0_attn_in['norm_g'], 'L0_attn_Wq': _L0_attn_in['Wq'], 'L0_attn_Wkv': _L0_attn_in['Wkv'], 'L0_attn_Wout': _L0_attn_in['Wout'], 'L0_attn_out_norm_g': _L0_attn_in['out_norm_g'], 'L0_ffn_wr': _L0_ffn_in['wr'], 'L0_ffn_w1': _L0_ffn_in['w1'], 'L0_ffn_b1': _L0_ffn_in['b1'], 'L0_ffn_w2': _L0_ffn_in['w2'], 'L0_ffn_b2': _L0_ffn_in['b2']}
    _x0 = _d['L0_attn_x']
    _d['L0_attn_x'] = jax.random.normal(jax.random.fold_in(jax.random.key(seed), 1), (4, 2048, 256), dtype=_x0.dtype)
    del _x0
    return _d

def reference(L0_attn_x, L0_attn_norm_g, L0_attn_Wq, L0_attn_Wkv, L0_attn_Wout, L0_attn_out_norm_g, L0_ffn_wr, L0_ffn_w1, L0_ffn_b1, L0_ffn_w2, L0_ffn_b2):

    def _L0_attn_ref(x, norm_g, Wq, Wkv, Wout, out_norm_g):
        import jax, jax.numpy as jnp
        import numpy as np
        import math
        EPS_LN = 1e-05
        SCALE = 16.0

        def layer_norm(x, g):
            mean = jnp.mean(x, axis=-1, keepdims=True)
            var = jnp.var(x, axis=-1, keepdims=True)
            return (x - mean) * jax.lax.rsqrt(var + EPS_LN) * g

        def l2norm(t):
            n = jnp.linalg.norm(t, axis=-1, keepdims=True)
            return t / jnp.maximum(n, 1e-12)
        b, n, dim = x.shape
        h = 8
        dh = Wkv.shape[-1] // 2
        xn = layer_norm(x, norm_g)
        q = xn @ Wq
        kv = xn @ Wkv
        k, v = (kv[..., :dh], kv[..., dh:])
        q = q.reshape(b, n, h, dh).transpose(0, 2, 1, 3)
        q = q * SCALE
        q = l2norm(q)
        k = l2norm(k)
        rs = math.sqrt(SCALE)
        q = q * rs
        k = k * rs
        sim = jnp.einsum('bhid,bjd->bhij', q, k)
        attn = jax.nn.softmax(sim.astype(jnp.float32), axis=-1).astype(sim.dtype)
        out = jnp.einsum('bhij,bjd->bhid', attn, v)
        out = out.transpose(0, 2, 1, 3).reshape(b, n, h * dh)
        out = out @ Wout
        return layer_norm(out, out_norm_g)

    def _L0_ffn_ref(hidden_states, wr, w1, b1, w2, b2):
        import jax, jax.numpy as jnp
        import numpy as np
        TOP_K = 2
        CAP_FACTOR = 1.25

        def _gelu(x):
            return 0.5 * x * (1.0 + jnp.tanh(jnp.sqrt(2.0 / jnp.pi) * (x + 0.044715 * x ** 3)))
        B, S, D = hidden_states.shape
        E = wr.shape[0]
        x = hidden_states.reshape(-1, D)
        T = x.shape[0]
        logits = x @ wr.T
        vals, idx = jax.lax.top_k(logits, TOP_K)
        sparse = jnp.full((T, E), -jnp.inf, dtype=logits.dtype)
        sparse = sparse.at[jnp.arange(T)[:, None], idx].set(vals)
        gating = jax.nn.softmax(sparse, axis=-1)
        cap = max(8, int(max(1, T * TOP_K // E) * CAP_FACTOR))
        mask = (idx[:, :, None] == jnp.arange(E)).any(axis=1)
        pos = jnp.cumsum(mask.astype(jnp.int32), axis=0) - 1
        keep = mask & (pos < cap)
        slot = jnp.where(keep, pos, cap)
        e_grid = jnp.broadcast_to(jnp.arange(E)[None, :], (T, E))
        t_grid = jnp.broadcast_to(jnp.arange(T)[:, None], (T, E))
        dispatch = jnp.full((E, cap + 1), T, dtype=jnp.int32)
        dispatch = dispatch.at[e_grid, slot].set(t_grid)[:, :cap]
        x_pad = jnp.concatenate([x, jnp.zeros((1, D), x.dtype)], axis=0)
        g_pad = jnp.concatenate([gating, jnp.zeros((1, E), gating.dtype)], axis=0)
        xg = x_pad[dispatch]
        h = _gelu(jnp.einsum('ecd,edf->ecf', xg, w1) + b1[:, None, :])
        y = jnp.einsum('ecf,efd->ecd', h, w2) + b2[:, None, :]
        g = g_pad[dispatch, jnp.arange(E)[:, None]]
        wy = y * g[..., None]
        out = jax.ops.segment_sum(wy.reshape(-1, D), dispatch.reshape(-1), num_segments=T + 1)[:T]
        return out.reshape(B, S, D)
    x = L0_attn_x
    xn = _layernorm(x, axis=-1)
    s = _L0_attn_ref(xn, L0_attn_norm_g, L0_attn_Wq, L0_attn_Wkv, L0_attn_Wout, L0_attn_out_norm_g)
    g = _silu(_L0_ffn_ref(xn, L0_ffn_wr, L0_ffn_w1, L0_ffn_b1, L0_ffn_w2, L0_ffn_b2))
    x = x + s * g
    return x

_drawn_inputs = setup_inputs


def setup_inputs(seed=0):
    import zlib

    import numpy as np

    out = dict(_drawn_inputs(seed))
    spreads = {'L0_attn_norm_g': (1.0, 0.583),
     'L0_attn_out_norm_g': (1.0, 0.6),
     'L0_ffn_b1': (0.0, 0.573),
     'L0_ffn_b2': (0.0, 0.1)}
    factors = {}
    for name, (base, spread) in spreads.items():
        noise = np.random.default_rng([zlib.crc32(name.encode()), seed]).standard_normal(out[name].shape)
        drawn = base * np.exp(spread * noise) if base else spread * noise
        out[name] = jnp.asarray(drawn.astype(out[name].dtype))
    for name, factor in factors.items():
        out[name] = (out[name] * factor).astype(out[name].dtype)
    return out
```

```python
from contextlib import ExitStack
from functools import partial

import numpy as np

import concourse.bass as bass
from concourse import mybir

F32 = mybir.dt.float32
F16 = mybir.dt.float16
BF16 = mybir.dt.bfloat16
I32 = mybir.dt.int32
ALU = mybir.AluOpType
ACT = mybir.ActivationFunctionType
AX = mybir.AxisListType.X

P = 128
GROUP_TILES = 4
TOP_K = 2
EPS = 1e-5
SCALE = 16.0
MIN_NORM = 1e-12
BANK_F32 = 512


class Stage:

    def __init__(self, engine, sem, by):
        self.engine, self.sem, self.by, self.count = engine, sem, by, 0


class Slot:

    def __init__(self, buf, stage=None):
        self.buf, self.stage, self.busy, self.freed = buf, stage, False, []

    def free(self, *tokens):
        self.busy, self.freed = False, list(tokens)


def take(slots, n=1):
    while sum(not s.busy for s in slots) < n:
        yield False
    taken = [s for s in slots if not s.busy][:n]
    for slot in taken:
        slots.remove(slot)
        slots.append(slot)
        slot.busy = True
    return taken[0] if n == 1 else taken


class Chains:

    def __init__(self, at_once):
        self.waiting, self.running, self.at_once = [], [], at_once

    def add(self, *chains):
        self.waiting += chains

    def advance(self, steps):
        blocked, asked = 0, steps
        while steps > 0 and (self.waiting or self.running) and blocked <= self.at_once:
            while self.waiting and len(self.running) < self.at_once:
                self.running.append(self.waiting.pop(0))
            chain = self.running.pop(0)
            try:
                moved = next(chain)
            except StopIteration:
                continue
            self.running.append(chain)
            if moved is False:
                blocked += 1
            else:
                blocked = 0
                steps -= 1
        return asked - steps

    def until(self, done):
        while not done():
            assert self.advance(1) or done(), "the side chains wait for each other"

    def finish(self):
        while self.waiting or self.running:
            assert self.advance(64) or not self.running, "the side chains wait for each other"


def build_program(nc, x, norm_g, Wq, Wkv, Wout, out_norm_g, wr, w1, b1, w2, b2, out):
    B, S, D = x.shape
    INNER = Wq.shape[1]
    DH = Wkv.shape[1] // 2
    H = INNER // DH
    E, _, F = w1.shape
    T = B * S
    NT = T // P
    GT = GROUP_TILES
    GP = GT * P
    NG = NT // GT
    BG = S // GP
    KB = S // P
    DC = D // P
    FC = F // P
    IC = INNER // P
    CAP = max(8, int(max(1, T * TOP_K // E) * 1.25))
    CT = CAP // P
    ROWS = E * CAP
    VW = 2 * DH + 1
    assert DH == 64 and D == 256 and GP == BANK_F32 and CAP % GP == 0 and NT * E == BANK_F32

    x_rows = x.rearrange("b s d -> (b s) d")
    out_rows = out.rearrange("b s d -> (b s) d")
    x_groups = x_rows.rearrange("(g j p) d -> g p j d", j=GT, p=P)
    x_tiles = x_rows.rearrange("(t p) d -> t p d", p=P)
    out_tiles = out_rows.rearrange("(t p) d -> t p d", p=P)

    xn_rows = nc.dram_tensor("xn_rows", [T, 2 * D], F16).ap()
    slot_token = nc.dram_tensor("slot_token", [ROWS + TOP_K * T, 1], I32).ap()
    expert_rows = nc.dram_tensor("expert_rows", [ROWS, D], F32).ap()
    attn_rows = nc.dram_tensor("attn_rows", [S, D], F32).ap()
    xn_groups = xn_rows.rearrange("(g j p) d -> g p j d", j=GT, p=P)
    expert_tiles = expert_rows.rearrange("(e p j) d -> e p j d", p=P, j=CT)
    attn_tiles = attn_rows.rearrange("(t p) d -> t p d", p=P)

    queues = {"sync": [], "tensor": [], "vector": [], "scalar": [], "gpsimd": []}

    with ExitStack() as ctx:
        def sb(name, shape, dt):
            return ctx.enter_context(nc.sbuf_tensor(name, shape, dt))

        def stage(engine, name, by=1):
            return Stage(engine, ctx.enter_context(nc.semaphore(name)), by)

        def do(st, emit, *needs):
            flat = []
            for n in needs:
                flat += n if isinstance(n, list) else [n]
            queues[st.engine].append((flat, emit, st))
            st.count += st.by
            return st, st.count

        banks = [ctx.enter_context(nc.psum_tensor(f"bank{i}", [P, BANK_F32], F32)) for i in range(8)]
        score_banks = [Slot(b) for b in banks[0:3]]
        acc_banks = [[Slot(banks[3]), Slot(banks[4])], [Slot(banks[5]), Slot(banks[6])]]
        side_banks = [Slot(banks[7])]

        ident32 = sb("ident32", [P, P], F32)
        ident16 = sb("ident16", [P, P], F16)
        identb = sb("identb", [P, P], BF16)
        upto = sb("upto", [P, P], BF16)
        onesb = sb("onesb", [P, P], BF16)
        minus_half = sb("minus_half", [P, H], F32)
        token_id = sb("token_id", [P, NT], I32)
        zero_ids = sb("zero_ids", [P, ROWS // P], I32)
        g_cols = sb("g_cols", [P, DC], F32)
        wr_sb = sb("wr_sb", [E, D], F32)
        wrT = sb("wrT", [P, DC, E], F32)
        b1_sb = sb("b1_sb", [E * FC, P], F32)
        b1T = sb("b1T", [P, E * FC], F32)
        out_g = sb("out_g", [P, D], F32)
        wq_hi = sb("wq_hi", [P, DC, INNER], BF16)
        wq_lo = sb("wq_lo", [P, DC, INNER], BF16)
        wkv_hi = sb("wkv_hi", [P, DC, 2 * DH], BF16)
        wkv_lo = sb("wkv_lo", [P, DC, 2 * DH], BF16)
        wo_hl = sb("wo_hl", [P, IC, 2 * D], BF16)
        raws = [Slot(sb(f"raw{i}", [P, 1024], F32), stage("sync", f"raw_loaded{i}", 16)) for i in range(2)]

        mean1 = sb("mean1", [P, NT, 2], F32)
        rstd1 = sb("rstd1", [P, NT], F32)
        mean2 = sb("mean2", [P, NT, 2], F32)
        rstd2 = sb("rstd2", [P, NT], F32)
        logits = sb("logits", [P, NT, E], F32)
        gate = [sb(f"gate{k}", [P, NT], F32) for k in range(TOP_K)]
        scatter_to = [sb(f"scatter_to{k}", [P, NT], I32) for k in range(TOP_K)]
        gather_from = [sb(f"gather_from{k}", [P, NT], I32) for k in range(TOP_K)]
        slot_ids = sb("slot_ids", [P, E, CT], I32)

        xin = [Slot(sb(f"xin{i}", [P, GT, D], F32), stage("sync", f"x_loaded{i}", 16)) for i in range(2)]
        xhl = [Slot(sb(f"xhl{i}", [P, GT, 2, D], F16), stage("sync", f"xn_stored{i}", 16)) for i in range(2)]
        bn_raw = [Slot(sb(f"bn_raw{i}", [P, GT, 6], F32)) for i in range(2)]
        small = [Slot(sb(f"small{i}", [P, 4, H], F32)) for i in range(4)]
        wide = [Slot(sb(f"wide{i}", [P, 512], F32)) for i in range(4)]
        xT = [sb(f"xT{i}", [P, 2 * DC, S], F16) for i in range(1)]
        kT = [sb(f"kT{i}", [P, 2, S], F16) for i in range(2)]
        vhl_row = [sb(f"vhl{i}", [P, KB * VW], BF16) for i in range(2)]
        vhl = [v[:, :].rearrange("p (k w) -> p k w", k=KB) for v in vhl_row]
        khl = [Slot(sb("khl", [P, GT, 2, 2, DH], F16))]
        qhl = [Slot(sb(f"qhl{i}", [P, H, 2, DH], F16)) for i in range(2)]
        qT = [sb(f"qT{i}", [P, H, GP], F16) for i in range(2)]
        att = [Slot(sb(f"att{i}", [P, GT, H, DH], F32)) for i in range(2)]
        oraw = [Slot(sb(f"oraw{i}", [P, GT, VW], F32)) for i in range(2)]
        ohl = [Slot(sb(f"ohl{i}", [P, 2, INNER], BF16)) for i in range(1)]
        oT = [Slot(sb(f"oT{i}", [P, 2 * IC, P], BF16)) for i in range(1)]
        s_rows = [Slot(sb(f"s_rows{i}", [P, D], F32), stage("sync", f"s_moved{i}", 16)) for i in range(3)]

        NP, NLO = 4, 3
        PAIR = 2 * BANK_F32
        arena = sb("arena", [P, 32 * 1024], mybir.dt.uint8)
        p_f32 = arena[:, 0:NP * PAIR * 4].bitcast(F32).rearrange("p (n c) -> p n c", n=NP)
        p_top = arena[:, 0:NP * PAIR * 4].bitcast(BF16).rearrange("p (n c t) -> p n c t", n=NP, t=2)
        p_lo = arena[:, NP * PAIR * 4:NP * PAIR * 4 + NLO * PAIR * 2].bitcast(BF16).rearrange("p (n c) -> p n c", n=NLO)
        h_hi = [arena[:, i * 8192:(i + 1) * 8192].bitcast(BF16).rearrange("p (f c) -> p f c", f=FC) for i in (0, 1)]
        h_lo = [arena[:, i * 8192:(i + 1) * 8192].bitcast(BF16).rearrange("p (f c) -> p f c", f=FC) for i in (2, 3)]
        w1_hi = [sb(f"w1_hi{i}", [P, DC, F], BF16) for i in range(2)]
        w1_lo = [sb(f"w1_lo{i}", [P, DC, F], BF16) for i in range(2)]
        w2_hl = [sb(f"w2_hl{i}", [P, FC, 2 * D], BF16) for i in range(2)]

        def flat(buf, dt):
            names = " ".join("abcd"[:len(buf.shape) - 1])
            return buf[tuple([slice(None)] * len(buf.shape))].rearrange(f"p {names} -> p ({names})").bitcast(dt)

        def cut(row, i, shape):
            n = int(np.prod(shape))
            piece = row[:, i * n:(i + 1) * n]
            return piece if len(shape) == 1 else piece.rearrange("p (a b) -> p a b", a=shape[0])

        xg = [Slot(cut(flat(att[0].buf, F16), i, [GT, 2 * D]), stage("gpsimd", f"x_gathered{i}", 16)) for i in range(2)]
        xgT = [Slot(cut(flat(kT[0], F16), i, [2 * DC, GP])) for i in range(2)]
        yout = [Slot(cut(flat(qT[1], F32), i, [GT, D]), stage("sync", f"y_stored{i}", 16)) for i in range(2)]
        ysum = [Slot(cut(flat(vhl_row[0], F32), i, [D])) for i in range(2)]
        b2_rows = [Slot(cut(flat(vhl_row[0], F32), 2 + i, [D]), stage("sync", f"b2_loaded{i}", 16)) for i in range(2)]
        h_f32 = [Slot(cut(flat(oraw[i].buf, F32), 0, [GP])) for i in range(2)]
        y_got = [Slot(cut(flat(w1_lo[0], F32), i, [TOP_K, D]), stage("gpsimd", f"y_gathered{i}", 16)) for i in range(2)]
        x_again = [Slot(cut(flat(w1_lo[1], F32), i, [D]), stage("sync", f"x_again_loaded{i}", 16)) for i in range(2)]
        res = [Slot(cut(flat(w1_lo[1], F32), 2 + i, [D]), stage("sync", f"out_stored{i}", 16)) for i in range(2)]

        loaded = stage("sync", "params_loaded", 16)
        pool_const = stage("gpsimd", "pool_const")
        dve_const = stage("vector", "dve_const")
        weights_hi = stage("scalar", "weights_hi")
        weights_lo = stage("vector", "weights_lo")
        pe_side = stage("tensor", "pe_side")
        act_side = stage("scalar", "act_side")
        dve_side = stage("vector", "dve_side")
        pool_side = stage("gpsimd", "pool_side")
        scattered = stage("gpsimd", "ids_scattered", 16)
        table_io = stage("sync", "table_io", 16)
        scored = stage("tensor", "scored")
        exped = stage("scalar", "exped")
        lowed = stage("vector", "lowed")
        weighted = stage("tensor", "weighted")
        acc_out = stage("scalar", "acc_out")
        turned = stage("tensor", "gathered_turned")
        turned_out = stage("scalar", "gathered_turned_out")
        hidden = stage("tensor", "hidden")
        gelued = stage("scalar", "gelued")
        hidden_lo = stage("vector", "hidden_lo")
        expert_out = stage("tensor", "expert_out")
        expert_sum = stage("vector", "expert_sum")

        def mm(o, w, m, start, stop, **kw):
            return partial(nc.tensor.matmul, o, w, m, start=start, stop=stop, **kw)

        def cast(o, i):
            return partial(nc.scalar.activation, o, i, ACT.Copy)

        t = do(pool_const, partial(nc.gpsimd.memset, ident32[:, :], 0.0))
        have_ident32 = do(pool_const, partial(nc.gpsimd.affine_select, out=ident32[:, :], in_=ident32[:, :], compare_op=ALU.not_equal, fill=1.0, base=0,
            pattern=[[-1, P]], channel_multiplier=1), t)
        t = do(pool_const, partial(nc.gpsimd.memset, upto[:, :], 1.0))
        have_upto = do(pool_const, partial(nc.gpsimd.affine_select, out=upto[:, :], in_=upto[:, :], compare_op=ALU.is_ge, fill=0.0, base=0,
            pattern=[[1, P]], channel_multiplier=-1), t)
        have_token_id = do(pool_const, partial(nc.gpsimd.iota, token_id[:, :], [[P, NT]], base=0, channel_multiplier=1))
        have_half = do(dve_const, partial(nc.vector.memset, minus_half[:, :], -0.5))
        have_ident16 = do(dve_const, partial(nc.vector.tensor_copy, ident16[:, :], ident32[:, :]), have_ident32)
        have_identb = do(dve_const, partial(nc.vector.tensor_copy, identb[:, :], ident32[:, :]), have_ident32)
        have_ones = do(dve_const, partial(nc.vector.memset, onesb[:, :], 1.0))
        have_zero_ids = do(dve_const, partial(nc.vector.memset, zero_ids[:, :], 0))

        do(loaded, partial(nc.sync.dma_start, g_cols[:, :], norm_g.rearrange("(c p) -> p c", p=P), allow_slow_non_contiguous=True))
        do(loaded, partial(nc.sync.dma_start, wr_sb[:, :], wr))
        do(loaded, partial(nc.sync.dma_start, b1_sb[:, :], b1.rearrange("e (f p) -> (e f) p", p=P)))
        have_params = do(loaded, partial(nc.sync.dma_start, out_g[:, :], out_norm_g.partition_broadcast(P)))
        table_zero = do(table_io, partial(nc.sync.dma_start, slot_token[0:ROWS, :].rearrange("(p j) o -> p (j o)", p=P), zero_ids[:, :]), have_zero_ids)

        def split_weight(src, width, parts, needs=()):
            slot = yield from take(raws)
            raw = slot.buf
            got = do(slot.stage, partial(nc.sync.dma_start, raw[:, 0:width].rearrange("p (a b) -> p a b", b=src.shape[2]), src), slot.freed)
            yield
            last = []
            for (a, b), hi, lo, scale in parts:
                if scale is None:
                    h = do(weights_hi, cast(hi, raw[:, a:b].rearrange(
                        "p (m n) -> p m n", n=hi.shape[-1])), got, *needs)
                    last.append(do(weights_lo, partial(nc.vector.tensor_tensor, lo, raw[:, a:b].rearrange("p (m n) -> p m n", n=hi.shape[-1]), hi, ALU.subtract), h, *needs))
                else:
                    h = do(weights_hi, partial(nc.scalar.activation, hi, raw[:, a:b], ACT.Copy, scale=scale),
                           got, have_params, *needs)
                    last.append(do(weights_lo, partial(nc.vector.scalar_tensor_tensor, out=lo, in0=raw[:, a:b], scalar=scale, in1=hi, op0=ALU.mult, op1=ALU.subtract), h, *needs))
                yield
            slot.free(*last)
            return last

        have = {}

        def attention_weights():
            r = yield from split_weight(
                Wkv.rearrange("(c p) n -> p c n", p=P), DC * 2 * DH,
                [((c * 2 * DH, (c + 1) * 2 * DH), wkv_hi[:, c, :], wkv_lo[:, c, :], g_cols[:, c:c + 1])
                 for c in range(DC)])
            have["wkv"] = r
            r = yield from split_weight(
                Wq.rearrange("(c p) n -> p c n", p=P), DC * INNER,
                [((c * INNER, (c + 1) * INNER), wq_hi[:, c, :], wq_lo[:, c, :], g_cols[:, c:c + 1])
                 for c in range(DC)])
            have["wq"] = r
            r = yield from split_weight(
                Wout.rearrange("(c p) n -> p c n", p=P), IC * D,
                [((0, IC * D), wo_hl[:, :, 0:D], wo_hl[:, :, D:2 * D], None)])
            have["wo"] = r

        def small_transposes():
            bank = yield from take(side_banks)
            ps = bank.buf
            for c in range(DC):
                a = do(pe_side, partial(nc.tensor.transpose, ps[:, c * E:(c + 1) * E], wr_sb[:, c * P:(c + 1) * P],
                                                           ident32[0:E, 0:E]), bank.freed, have_params, have_ident32)
            b = do(pe_side, partial(nc.tensor.transpose, ps[:, 64:64 + E * FC], b1_sb[:, :], ident32[0:E * FC, 0:E * FC]))
            yield
            c1 = do(act_side, cast(wrT[:, :, :], ps[:, 0:DC * E].rearrange("p (c n) -> p c n", c=DC)), a, b)
            c2 = do(act_side, cast(b1T[:, :], ps[:, 64:64 + E * FC]), b)
            bank.free(c2)
            have["wrT"], have["b1T"] = c1, c2
            yield

        stats_done = {}
        xn_stored = {}
        logits_done = {}

        def normalise(src, dst, mean, rstd, g, *needs):
            for j in range(GT):
                t = do(dve_side, partial(nc.vector.tensor_scalar, dst[:, j, :], src[:, j, :], mean[:, g * GT + j, 0:1], rstd[:, g * GT + j:g * GT + j + 1],
                    ALU.subtract, ALU.mult), *needs)
            return t

        def moments(src, mean, rstd, g, *needs):
            bn = yield from take(bn_raw)
            sm = yield from take(small)
            for j in range(GT):
                t = do(dve_side, partial(nc.vector.bn_stats, bn.buf[:, j, :], src[:, j, :]), bn.freed, *needs)
            for j in range(GT):
                t2 = do(dve_side, partial(nc.vector.bn_aggr, mean[:, g * GT + j, :], bn.buf[:, j, :]), t)
            bn.free(t2)
            t = do(dve_side, partial(nc.vector.tensor_scalar, sm.buf[:, 0, 0:GT], mean[:, g * GT:(g + 1) * GT, 1], EPS, None,
                                                       ALU.add), t2, sm.freed)
            yield
            t = do(pool_side, partial(nc.gpsimd.tensor_tensor, rstd[:, g * GT:(g + 1) * GT], sm.buf[:, 0, 0:GT],
                                                        minus_half[:, 0:GT], ALU.pow), t, have_half)
            sm.free(t)
            yield
            return t

        def statistics(g):
            xs = yield from take(xin)
            got = do(xs.stage, partial(nc.sync.dma_start, xs.buf[:, :, :], x_groups[g]), xs.freed)
            yield
            r = yield from moments(xs.buf, mean1, rstd1, g, got)
            xn = normalise(xs.buf, xs.buf, mean1, rstd1, g, r)
            yield
            r2 = yield from moments(xs.buf, mean2, rstd2, g, xn)
            stats_done[g] = r2
            hl = yield from take(xhl)
            hi = do(act_side, cast(hl.buf[:, :, 0, :], xs.buf[:, :, :]), xn, hl.freed)
            yield
            lo = do(dve_side, partial(nc.vector.tensor_tensor, hl.buf[:, :, 1, :], xs.buf[:, :, :], hl.buf[:, :, 0, :],
                                                        ALU.subtract), hi)
            st = do(hl.stage, partial(nc.sync.dma_start, xn_groups[g], hl.buf[:, :, :, :].rearrange(
                "p j k d -> p j (k d)")), lo)
            hl.free(st)
            xn_stored[g] = st
            yield
            turned_x = []
            xts = yield from take(wide, DC)
            for c, xt in enumerate(xts):
                bank = yield from take(side_banks)
                for j in range(GT):
                    t = do(pe_side, partial(nc.tensor.transpose, bank.buf[:, j * P:(j + 1) * P], xs.buf[:, j, c * P:(c + 1) * P], ident32[:, :]),
                        bank.freed, xn, have_ident32)
                yield
                t = do(act_side, cast(xt.buf[:, :], bank.buf[:, :]), t, xt.freed)
                bank.free(t)
                turned_x.append((xt, t))
                yield
            xs.free(lo, turned_x[-1][1], r2)
            bank = yield from take(side_banks)
            for j in range(GT):
                for c, (xt, ready) in enumerate(turned_x):
                    t = do(pe_side, mm(bank.buf[:, j * E:(j + 1) * E], xt.buf[:, j * P:(j + 1) * P], wrT[:, c, :],
                        start=(j == 0 and c == 0), stop=(c == DC - 1), skip_group_check=True),
                        bank.freed, ready, have["wrT"])
            for xt, _ in turned_x:
                xt.free(t)
            yield
            t = do(act_side, cast(logits[:, g * GT:(g + 1) * GT, :], bank.buf[:, 0:GT * E].rearrange(
                "p (j n) -> p j n", j=GT)), t)
            bank.free(t)
            logits_done[g] = t
            yield

        def work(buf, n):
            v = buf[:, :, :].rearrange("p a b -> p (a b)").bitcast(F32)
            return [v[:, i * 512:(i + 1) * 512].rearrange("p (t e) -> p t e", e=E) for i in range(n)]

        route_done = {}

        def route():
            while len(logits_done) < NG:
                yield False
            iota_i = work(w2_hl[1], 4)[0].bitcast(I32)
            first, second, mask_f, row, keep, scan_a, scan_b, tmp = work(w2_hl[0], 4) + work(w1_hi[0], 2) + work(w1_lo[0], 2)
            prefer, base_row, key, total = work(w1_hi[1], 2) + work(w1_lo[1], 2)
            vecs = work(w2_hl[1], 4)[1].rearrange("p t e -> p (t e)")
            trash_v = work(w2_hl[1], 4)[2].rearrange("p t e -> p (t e)")
            m1, m2, r, dd, den, inv, pk, kk = [vecs[:, i * NT:(i + 1) * NT] for i in range(8)]
            trash = [trash_v[:, k * NT:(k + 1) * NT] for k in range(TOP_K)]
            mask16 = work(w2_hl[1], 4)[3].bitcast(BF16).rearrange("p t e -> p (t e)")[:, 0:NT * E]

            last = [list(logits_done.values()) + [have_half]]

            def v(emit, *needs):
                last[0] = [do(dve_side, emit, last[0], *needs)]

            def wide_of(a):
                return a.unsqueeze(2).to_broadcast([P, NT, E])

            i1 = do(pool_side, partial(nc.gpsimd.iota, iota_i, [[0, NT], [-1, E]], base=E, channel_multiplier=0), last[0])
            v(partial(nc.vector.tensor_copy, prefer, iota_i), i1)
            i2 = do(pool_side, partial(nc.gpsimd.iota, iota_i, [[0, NT], [CAP, E]], base=0, channel_multiplier=0), last[0])
            v(partial(nc.vector.tensor_copy, base_row, iota_i), i2)
            yield
            for k in range(TOP_K):
                ii = iota_i.rearrange("p t e -> p (t e)")[:, 0:NT]
                i3 = do(pool_side, partial(nc.gpsimd.iota, ii, [[P, NT]], base=ROWS + k * T, channel_multiplier=1), last[0])
                v(partial(nc.vector.tensor_copy, trash[k], ii), i3)
                yield
            for src, best, hot in ((logits[:, :, :], m1, first), (tmp, m2, second)):
                v(partial(nc.vector.tensor_reduce, best, src, AX, ALU.max))
                yield
                v(partial(nc.vector.tensor_tensor, key, src, wide_of(best), ALU.is_equal))
                yield
                v(partial(nc.vector.tensor_tensor, key, key, prefer, ALU.mult))
                yield
                v(partial(nc.vector.tensor_reduce, r, key, AX, ALU.max))
                yield
                v(partial(nc.vector.tensor_tensor, hot, key, wide_of(r), ALU.is_equal))
                yield
                if src is not tmp:
                    v(partial(nc.vector.scalar_tensor_tensor, out=tmp.rearrange("p t e -> p (t e)"), in0=first.rearrange("p t e -> p (t e)"), scalar=-3e38,
                        in1=logits[:, :, :].rearrange("p t e -> p (t e)"), op0=ALU.mult, op1=ALU.add))
                    yield
            v(partial(nc.vector.tensor_tensor, dd, m2, m1, ALU.subtract))
            yield
            ex = do(act_side, partial(nc.scalar.activation, pk, dd, ACT.Exp), last[0])
            last[0] = [ex]
            v(partial(nc.vector.tensor_scalar, den, pk, 1.0, None, ALU.add))
            v(partial(nc.vector.reciprocal, gate[0][:, :], den))
            v(partial(nc.vector.tensor_tensor, gate[1][:, :], gate[0][:, :], pk, ALU.mult))
            yield
            v(partial(nc.vector.tensor_tensor, mask_f, first, second, ALU.add))
            yield
            v(partial(nc.vector.tensor_copy, mask16.rearrange("p (t e) -> p t e", e=E), mask_f))
            yield
            bank = yield from take(side_banks)
            tot = do(pe_side, mm(bank.buf[:, :], onesb[:, :], mask16, True, True),
                     last[0], bank.freed, have_ones)
            yield
            v(partial(nc.vector.tensor_copy, total, bank.buf[:, :].rearrange("p (t e) -> p t e", e=E)), tot)
            inc = do(pe_side, mm(bank.buf[:, :], upto[:, :], mask16, True, True), last[0], have_upto)
            yield
            v(partial(nc.vector.tensor_copy, row, bank.buf[:, :].rearrange("p (t e) -> p t e", e=E)), inc)
            bank.free(*last[0])
            yield
            a, b, step = total, scan_a, 1
            while step < NT:
                v(partial(nc.vector.tensor_copy, b[:, 0:step, :], a[:, 0:step, :]))
                v(partial(nc.vector.tensor_tensor, b[:, step:NT, :], a[:, step:NT, :], a[:, 0:NT - step, :], ALU.add))
                yield
                a, b, step = b, (scan_b if a is total else a), step * 2
            v(partial(nc.vector.tensor_tensor, row, row, a, ALU.add))
            yield
            v(partial(nc.vector.tensor_tensor, row, row, total, ALU.subtract))
            yield
            v(partial(nc.vector.tensor_scalar, row, row, -1.0, None, ALU.add))
            yield
            v(partial(nc.vector.tensor_scalar, keep, row, float(CAP), None, ALU.is_lt))
            yield
            v(partial(nc.vector.tensor_tensor, row, row, base_row, ALU.add))
            yield
            for k, hot in ((0, first), (1, second)):
                v(partial(nc.vector.tensor_tensor, tmp, hot, row, ALU.mult))
                yield
                v(partial(nc.vector.tensor_reduce, pk, tmp, AX, ALU.add))
                yield
                v(partial(nc.vector.tensor_tensor, tmp, hot, keep, ALU.mult))
                yield
                v(partial(nc.vector.tensor_reduce, kk, tmp, AX, ALU.add))
                v(partial(nc.vector.tensor_tensor, gate[k][:, :], gate[k][:, :], kk, ALU.mult))
                v(partial(nc.vector.tensor_tensor, dd, pk, trash[k], ALU.subtract))
                v(partial(nc.vector.tensor_tensor, dd, dd, kk, ALU.mult))
                yield
                v(partial(nc.vector.tensor_tensor, dd, dd, trash[k], ALU.add))
                v(partial(nc.vector.tensor_copy, scatter_to[k][:, :], dd))
                v(partial(nc.vector.tensor_tensor, dd, pk, kk, ALU.mult))
                v(partial(nc.vector.tensor_copy, gather_from[k][:, :], dd))
                yield
            route_done["all"] = last[0]
            for t in range(NT):
                for k in range(TOP_K):
                    done = do(scattered, partial(nc.gpsimd.indirect_dma_start, slot_token, bass.IndirectOffsetOnAxis(scatter_to[k][:, t:t + 1], 0),
                        token_id[:, t:t + 1], None), last[0], table_zero, have_token_id)
                    yield
            route_done["ids"] = do(table_io, partial(nc.sync.dma_start, slot_ids[:, :, :], slot_token[0:ROWS, :].rearrange("(e p j) o -> p e (j o)", p=P, j=CT)), done)
            yield

        kv_done = {}
        xT_used = {}
        kv_used = {}

        def turn(bank, dst_of, src_tiles, ident, dt, needs):
            view = bank.buf[:, :].bitcast(dt)
            for i, s in enumerate(src_tiles):
                t = do(pe_side, partial(nc.tensor.transpose, view[:, i * P:(i + 1) * P], s, ident[:, :]),
                       bank.freed, *needs)
            return t

        def prepare_kv(g):
            b, gi = divmod(g, BG)
            while g not in stats_done or "wkv" not in have:
                yield False
            while b > 0 and len(xT_used.get(b - 1, [])) < BG:
                yield False
            xs = yield from take(xin)
            got = do(xs.stage, partial(nc.sync.dma_start, xs.buf[:, :, :], x_groups[g]), xs.freed)
            yield
            t = normalise(xs.buf, xs.buf, mean1, rstd1, g, got, stats_done[g])
            yield
            xn2 = normalise(xs.buf, xs.buf, mean2, rstd2, g, t)
            yield
            hl = yield from take(xhl)
            hi = do(act_side, cast(hl.buf[:, :, 0, :], xs.buf[:, :, :]), xn2, hl.freed)
            yield
            lo = do(dve_side, partial(nc.vector.tensor_tensor, hl.buf[:, :, 1, :], xs.buf[:, :, :], hl.buf[:, :, 0, :],
                                                        ALU.subtract), hi)
            xs.free(lo)
            yield
            old = xT_used.get(b - 1, [])
            for half in range(2):
                bank = yield from take(side_banks)
                tiles = [hl.buf[:, 2 * half + j, k, c * P:(c + 1) * P] for k in range(2) for c in range(DC) for j in range(2)]
                t = turn(bank, None, tiles, ident16, F16, [lo, have_ident16])
                yield
                at = gi * GP + half * 2 * P
                ready = do(act_side, cast(xT[0][:, :, at:at + 2 * P], bank.buf[:, :].bitcast(F16).rearrange(
                    "p (k c) -> p k c", k=2 * DC)), t, *old)
                bank.free(ready)
                yield
            hl.free(t)
            kv, sq = yield from take(wide, 2)
            bank = yield from take(side_banks)
            W = 2 * DH
            for j in range(GT):
                at = gi * GP + j * P
                n = 0
                for kind, w in ((0, wkv_hi), (0, wkv_lo), (1, wkv_hi)):
                    for c in range(DC):
                        t = do(pe_side, mm(bank.buf[:, j * W:(j + 1) * W], xT[0][:, kind * DC + c, at:at + P], w[:, c, :],
                            start=(j == 0 and n == 0), stop=(n == 3 * DC - 1), skip_group_check=True),
                            ready, bank.freed, have["wkv"])
                        n += 1
            yield
            kvv = kv.buf[:, :].rearrange("p (j n) -> p j n", j=GT)
            t = do(act_side, cast(kv.buf[:, :], bank.buf[:, :]), t, kv.freed)
            bank.free(t)
            yield
            k_f, v_f = kvv[:, :, 0:DH], kvv[:, :, DH:W]
            V = vhl[b % 2][:, gi * GT:(gi + 1) * GT, :]
            do(dve_side, partial(nc.vector.memset, V[:, :, DH:DH + 1], 1.0), *kv_used.get(b - 2, []))
            vh = do(dve_side, partial(nc.vector.tensor_copy, V[:, :, 0:DH], v_f), t, *kv_used.get(b - 2, []))
            vl = do(dve_side, partial(nc.vector.tensor_tensor, V[:, :, DH + 1:VW], v_f, V[:, :, 0:DH], ALU.subtract), vh)
            yield
            sm = yield from take(small)
            sqv = sq.buf[:, 0:GT * DH].rearrange("p (j n) -> p j n", j=GT)
            t = do(dve_side, partial(nc.vector.tensor_tensor, sqv, k_f, k_f, ALU.mult), t, sq.freed)
            t = do(dve_side, partial(nc.vector.tensor_reduce, sm.buf[:, 0, 0:GT], sqv, AX, ALU.add), t, sm.freed)
            t = do(dve_side, partial(nc.vector.tensor_scalar, sm.buf[:, 1, 0:GT], sm.buf[:, 0, 0:GT], 1 / SCALE,
                                                       MIN_NORM ** 2 / SCALE, ALU.mult, ALU.max), t)
            yield
            t = do(pool_side, partial(nc.gpsimd.tensor_tensor, sm.buf[:, 2, 0:GT], sm.buf[:, 1, 0:GT], minus_half[:, 0:GT],
                                                        ALU.pow), t)
            yield
            yield
            t = do(dve_side, partial(nc.vector.tensor_tensor, sqv, k_f, sm.buf[:, 2, 0:GT].unsqueeze(2).to_broadcast([P, GT, DH]),
                                                       ALU.mult), t)
            kv.free(t, vl)
            sm.free(t)
            kn = yield from take(khl)
            twice = sqv.unsqueeze(2).to_broadcast([P, GT, 2, DH])
            t = do(dve_side, partial(nc.vector.tensor_copy, kn.buf[:, :, 0, :, :], twice), t, kn.freed)
            t = do(dve_side, partial(nc.vector.tensor_tensor, kn.buf[:, :, 1, :, :], twice, kn.buf[:, :, 0, :, :],
                                                       ALU.subtract), t)
            sq.free(t)
            yield
            bank = yield from take(side_banks)
            tiles = [kn.buf[:, j, k, :, :].rearrange("p a b -> p (a b)") for k in range(2) for j in range(GT)]
            t = turn(bank, None, tiles, ident16, F16, [t, have_ident16])
            kn.free(t)
            yield
            t = do(act_side, cast(kT[b % 2][:, :, gi * GP:(gi + 1) * GP], bank.buf[:, :].bitcast(
                F16).rearrange("p (k c) -> p k c", k=2)), t, *kv_used.get(b - 2, []))
            bank.free(t)
            kv_done[g] = [t, vl, ready]
            yield

        q_done = {}
        q_used = {}

        def prepare_q(g):
            b, gi = divmod(g, BG)
            while g not in kv_done or "wq" not in have:
                yield False
            while g >= 2 and g - 2 not in q_used:
                yield False
            for j in range(GT):
                at = gi * GP + j * P
                qf, sq = yield from take(wide, 2)
                bank = yield from take(side_banks)
                n = 0
                for kind, w in ((0, wq_hi), (0, wq_lo), (1, wq_hi)):
                    for c in range(DC):
                        t = do(pe_side, mm(bank.buf[:, :], xT[0][:, kind * DC + c, at:at + P], w[:, c, :],
                            start=(n == 0), stop=(n == 3 * DC - 1)), kv_done[g], bank.freed, have["wq"])
                        n += 1
                last_read = t
                yield
                t = do(act_side, cast(qf.buf[:, :], bank.buf[:, :]), t, qf.freed)
                bank.free(t)
                yield
                sm = yield from take(small)
                qv, sqv = [a.buf[:, :].rearrange("p (h n) -> p h n", h=H) for a in (qf, sq)]
                t = do(pool_side, partial(nc.gpsimd.tensor_tensor, sq.buf[:, :], qf.buf[:, :], qf.buf[:, :], ALU.mult), t, sq.freed)
                yield
                yield
                t = do(dve_side, partial(nc.vector.tensor_reduce, sm.buf[:, 0, :], sqv, AX, ALU.add), t, sm.freed)
                t = do(dve_side, partial(nc.vector.tensor_scalar, sm.buf[:, 1, :], sm.buf[:, 0, :], SCALE ** 2 / (SCALE ** 3), MIN_NORM ** 2 / SCALE ** 3,
                    ALU.mult, ALU.max), t)
                yield
                t = do(pool_side, partial(nc.gpsimd.tensor_tensor, sm.buf[:, 2, :], sm.buf[:, 1, :], minus_half[:, :], ALU.pow), t)
                yield
                yield
                t = do(dve_side, partial(nc.vector.tensor_tensor, sqv, qv, sm.buf[:, 2, :].unsqueeze(2).to_broadcast([P, H, DH]),
                                                           ALU.mult), t)
                qf.free(t)
                sm.free(t)
                yield
                hl = yield from take(qhl)
                t = do(act_side, cast(hl.buf[:, :, 0, :], sqv), t, hl.freed)
                yield
                t = do(dve_side, partial(nc.vector.tensor_tensor, hl.buf[:, :, 1, :], sqv, hl.buf[:, :, 0, :], ALU.subtract), t)
                sq.free(t)
                yield
                bank = yield from take(side_banks)
                t = turn(bank, None, [hl.buf[:, h, :, :].rearrange("p a b -> p (a b)") for h in range(H)],
                         ident16, F16, [t, have_ident16])
                hl.free(t)
                yield
                t = do(act_side, cast(qT[g % 2][:, :, j * P:(j + 1) * P], bank.buf[:, :].bitcast(
                    F16).rearrange("p (h c) -> p h c", h=H)), t, q_used.get(g - 2, []))
                bank.free(t)
                yield
            q_done[g] = [t]
            xT_used.setdefault(b, []).append(last_read)

        p_free = [[] for _ in range(NP)]
        lo_free = [[] for _ in range(NLO)]
        att_done = {}
        pairs_made = [0]
        acc_made = [0]

        def attention(g, side, steps_per_pair):
            b, gi = divmod(g, BG)
            side.until(lambda: g in q_done and all(b * BG + i in kv_done for i in range(BG)))
            kt, V, q = kT[b % 2], vhl[b % 2], qT[g % 2]
            while att[g % 2].busy:
                side.advance(1)
            att[g % 2].busy = True
            rows = att[g % 2]
            ready = q_done[g] + [t for i in range(BG) for t in kv_done[b * BG + i]]
            NPAIR = KB // 2
            pending = []
            after = []
            last_score = None

            def scores(h, pr):
                n = pairs_made[0]
                pairs_made[0] += 1
                slot = n % NP
                ex = []
                for i in range(2):
                    kb = 2 * pr + i
                    bank = score_banks.pop(0)
                    score_banks.append(bank)
                    for part in range(2):
                        t = do(scored, mm(bank.buf[:, :], kt[:, part, kb * P:(kb + 1) * P], q[:, h, :], part == 0, part == 1),
                            bank.freed, ready)
                    x_t = do(exped, partial(nc.scalar.activation, p_f32[:, slot, i * BANK_F32:(i + 1) * BANK_F32], bank.buf[:, :], ACT.Exp), t, p_free[slot])
                    bank.free(x_t)
                    ex.append(x_t)
                    if i == 0:
                        yield t
                lo_slot = n % NLO
                low = do(lowed, partial(nc.vector.tensor_tensor, p_lo[:, lo_slot, :], p_f32[:, slot, :], p_top[:, slot, :, 1], ALU.subtract), ex, lo_free[lo_slot])
                pending.append((h, pr, slot, lo_slot, ex, low))
                yield t

            def weigh(item):
                h, pr, slot, lo_slot, ex, low = item
                accs = acc_banks[acc_made[0] % 2]
                for i in range(2):
                    kb = 2 * pr + i
                    for qb in range(GT):
                        bank = accs[qb // 2]
                        at = (qb % 2) * VW
                        cols = slice(i * BANK_F32 + qb * P, i * BANK_F32 + (qb + 1) * P)
                        do(weighted, mm(bank.buf[:, at:at + VW], p_top[:, slot, cols, 1], V[:, kb, :],
                            start=(kb == 0 and qb % 2 == 0), stop=False, skip_group_check=True), ex, bank.freed)
                        t = do(weighted, mm(bank.buf[:, at:at + DH + 1], p_lo[:, lo_slot, cols], V[:, kb, 0:DH + 1],
                            start=False, stop=(kb == KB - 1), skip_group_check=True), low)
                    if i == 0:
                        yield
                p_free[slot] = [t]
                lo_free[lo_slot] = [t]
                if pr == NPAIR - 1:
                    acc_made[0] += 1
                    o = next(s for s in oraw if not s.busy)
                    oraw.remove(o)
                    oraw.append(o)
                    o.busy = True
                    for k, bank in enumerate(accs):
                        c = do(acc_out, cast(o.buf[:, 2 * k:2 * k + 2, :], bank.buf[:, 0:2 * VW].rearrange("p (a b) -> p a b", a=2)),
                            t, o.freed)
                        bank.free(c)
                    after.append((h, o, c))
                yield

            def divide(h, o, copied):
                sm = next(s for s in oden if not s.busy)
                s = do(pool_side, partial(nc.gpsimd.tensor_tensor, osum.buf[:, :, :], o.buf[:, :, 0:DH], o.buf[:, :, DH + 1:VW],
                                                            ALU.add), copied, osum.freed)
                r = do(dve_side, partial(nc.vector.reciprocal, sm.buf[:, :, :], o.buf[:, :, DH:DH + 1]), copied, sm.freed)
                yield
                t = do(dve_side, partial(nc.vector.tensor_tensor, rows.buf[:, :, h, :], osum.buf[:, :, :],
                                                           sm.buf[:, :, :].to_broadcast([P, GT, DH]), ALU.mult),
                       s, r, rows.freed)
                osum.free(t)
                sm.free(t)
                o.free(t)
                att_done[g] = t
                yield

            fins = []
            for h in range(H):
                for pr in range(NPAIR):
                    sc = scores(h, pr)
                    last_score = next(sc)
                    w = weigh(pending.pop(0)) if len(pending) >= 2 else None
                    if w:
                        next(w)
                    last_score = next(sc)
                    if w:
                        for _ in w:
                            pass
                    for f in list(fins):
                        if next(f, "end") == "end":
                            fins.remove(f)
                    while after:
                        fins.append(divide(*after.pop(0)))
                    side.advance(steps_per_pair)
            q_used[g] = [last_score]
            while pending:
                for _ in weigh(pending.pop(0)):
                    pass
                side.advance(1)
            for f in fins + [divide(*a) for a in after]:
                for _ in f:
                    pass
            kv_used.setdefault(b, []).append(weighted_token())
            if gi == BG - 1:
                kv_used[b].append(last_score)

        def weighted_token():
            return weighted, weighted.count

        osum = Slot(sb("osum", [P, GT, DH], F32))
        oden = [Slot(sb("oden", [P, GT, 1], F32))]

        s_done = {}

        def project_out(g):
            rows = att[g % 2]
            ready = att_done[g]
            while "wo" not in have:
                yield False
            for j in range(GT):
                t_id = g * GT + j
                hl = yield from take(ohl)
                src = rows.buf[:, j, :, :].rearrange("p h d -> p (h d)")
                t = do(act_side, cast(hl.buf[:, 0, :], src), ready, hl.freed)
                yield
                t = do(dve_side, partial(nc.vector.tensor_tensor, hl.buf[:, 1, :], src, hl.buf[:, 0, :], ALU.subtract), t)
                if j == GT - 1:
                    rows.free(t)
                yield
                ot = yield from take(oT)
                s = yield from take(s_rows)
                wd = yield from take(wide)
                bank = yield from take(side_banks)
                t = turn(bank, None, [hl.buf[:, k, c * P:(c + 1) * P] for k in range(2) for c in range(IC)],
                         identb, BF16, [t, have_identb])
                hl.free(t)
                yield
                t = do(act_side, cast(ot.buf[:, :, :], bank.buf[:, :].bitcast(BF16).rearrange(
                    "p (k c) -> p k c", k=2 * IC)), t, ot.freed)
                bank.free(t)
                yield
                bank = yield from take(side_banks)
                for c in range(IC):
                    do(pe_side, mm(bank.buf[:, :], ot.buf[:, c, :], wo_hl[:, c, :], c == 0, False,
                                                  skip_group_check=True), t, bank.freed, have["wo"])
                for c in range(IC):
                    m = do(pe_side, mm(bank.buf[:, 0:D], ot.buf[:, IC + c, :], wo_hl[:, c, 0:D],
                                                      False, c == IC - 1, skip_group_check=True))
                ot.free(m)
                yield
                a = do(act_side, cast(wd.buf[:, 0:D], bank.buf[:, D:2 * D]), m, wd.freed)
                yield
                t = do(dve_side, partial(nc.vector.tensor_tensor, wd.buf[:, D:2 * D], bank.buf[:, 0:D], wd.buf[:, 0:D], ALU.add), a)
                bank.free(t)
                bn = yield from take(bn_raw)
                sm = yield from take(small)
                o = wd.buf[:, D:2 * D]
                t = do(dve_side, partial(nc.vector.bn_stats, bn.buf[:, 0, :], o), t, bn.freed)
                t = do(dve_side, partial(nc.vector.bn_aggr, sm.buf[:, 0, 0:2], bn.buf[:, 0, :]), t, sm.freed)
                bn.free(t)
                t = do(dve_side, partial(nc.vector.tensor_scalar, sm.buf[:, 1, 0:1], sm.buf[:, 0, 1:2], EPS, None, ALU.add), t)
                yield
                t = do(pool_side, partial(nc.gpsimd.tensor_tensor, sm.buf[:, 2, 0:1], sm.buf[:, 1, 0:1], minus_half[:, 0:1],
                                                            ALU.pow), t)
                yield
                yield
                t = do(dve_side, partial(nc.vector.tensor_scalar, wd.buf[:, 0:D], o, sm.buf[:, 0, 0:1], sm.buf[:, 2, 0:1],
                                                           ALU.subtract, ALU.mult), t)
                sm.free(t)
                yield
                t = do(pool_side, partial(nc.gpsimd.tensor_tensor, s.buf[:, :], wd.buf[:, 0:D], out_g[:, :], ALU.mult),
                       t, s.freed, have_params)
                wd.free(t)
                yield
                if experts_recorded:
                    side_chains.waiting.insert(0, combine(t_id, s, t))
                else:
                    t = do(s.stage, partial(nc.sync.dma_start, attn_tiles[t_id], s.buf[:, :]), t)
                    s.free(t)
                    s_done[t_id] = t
                    side_chains_after.append(t_id)
                    yield

        side_chains_after = []
        experts_recorded = []

        def combine(t_id, s, s_ready):
            if s is None:
                s = yield from take(s_rows)
                s_ready = do(s.stage, partial(nc.sync.dma_start, s.buf[:, :], attn_tiles[t_id]), s.freed, s_done[t_id])
            xa = yield from take(x_again)
            x_ready = do(xa.stage, partial(nc.sync.dma_start, xa.buf[:, :], x_tiles[t_id]), xa.freed)
            y = yield from take(y_got)
            for k in range(TOP_K):
                y_ready = do(y.stage, partial(nc.gpsimd.indirect_dma_start, y.buf[:, k, :], None, expert_rows, bass.IndirectOffsetOnAxis(gather_from[k][:, t_id:t_id + 1], 0)),
                    y.freed, experts_recorded[0], route_done["all"])
            for _ in range(6):
                yield
            r = yield from take(res)
            wd = yield from take(wide)
            f, w = wd.buf[:, 0:D], wd.buf[:, D:2 * D]
            t = do(dve_side, partial(nc.vector.tensor_scalar, f, y.buf[:, 0, :], gate[0][:, t_id:t_id + 1], None, ALU.mult),
                   y_ready, wd.freed)
            t = do(dve_side, partial(nc.vector.scalar_tensor_tensor, out=f, in0=y.buf[:, 1, :], scalar=gate[1][:, t_id:t_id + 1], in1=f, op0=ALU.mult, op1=ALU.add), t)
            y.free(t)
            yield
            a = do(act_side, partial(nc.scalar.activation, w, f, ACT.Exp, scale=-1.0), t)
            sf = do(pool_side, partial(nc.gpsimd.tensor_tensor, s.buf[:, :], s.buf[:, :], f, ALU.mult), t, s_ready)
            yield
            t = do(dve_side, partial(nc.vector.tensor_scalar, w, w, 1.0, None, ALU.add), a)
            t = do(dve_side, partial(nc.vector.reciprocal, w, w), t)
            yield
            t = do(pool_side, partial(nc.gpsimd.tensor_tensor, w, s.buf[:, :], w, ALU.mult), t, sf)
            s.free(t)
            t = do(pool_side, partial(nc.gpsimd.tensor_tensor, r.buf[:, :], w, xa.buf[:, :], ALU.add), t, x_ready, r.freed)
            xa.free(t)
            wd.free(t)
            yield
            t = do(r.stage, partial(nc.sync.dma_start, out_tiles[t_id], r.buf[:, :]), t)
            r.free(t)
            yield

        w_ready = {}
        w_used = {}

        def expert_weights(ex):
            while "all" not in route_done:
                yield False
            while ex >= 2 and ex - 2 not in w_used:
                yield False
            i = ex % 2
            needs = w_used.get(ex - 2, []) + route_done["all"]
            while 0 not in kv_used or len(kv_used[0]) < BG + 1:
                yield False
            r = []
            w1_src = w1[ex].rearrange("(c p) f -> p c f", p=P)
            w2_src = w2[ex].rearrange("(f p) d -> p f d", p=P)
            for c in range(DC):
                r += yield from split_weight(w1_src[:, c:c + 1, :], F, [
                    ((0, F), w1_hi[i][:, c:c + 1, :], w1_lo[i][:, c:c + 1, :], None)], needs)
            for c in range(2):
                fs = slice(c * FC // 2, (c + 1) * FC // 2)
                r += yield from split_weight(w2_src[:, fs, :], FC // 2 * D, [
                    ((0, FC // 2 * D), w2_hl[i][:, fs, 0:D], w2_hl[i][:, fs, D:2 * D], None)], needs)
            bb = b2_rows[i]
            r.append(do(bb.stage, partial(nc.sync.dma_start, bb.buf[:, :], b2[ex].partition_broadcast(P)), needs, kv_used[0]))
            w_ready[ex] = r
            yield

        NQ = CT // GT
        FG = E * NQ
        gathered = {}
        turned_x = {}

        def gather(fg):
            ex, q = divmod(fg, NQ)
            s = xg[fg % 2]
            for j in range(GT):
                t = do(s.stage, partial(nc.gpsimd.indirect_dma_start, s.buf[:, j, :], None, xn_rows, bass.IndirectOffsetOnAxis(slot_ids[:, ex, q * GT + j:q * GT + j + 1], 0)),
                    s.freed, route_done["ids"], list(xn_stored.values()))
            gathered[fg] = t

        turn_banks = acc_banks[1]

        def turn_gathered(fg):
            s, d = xg[fg % 2], xgT[fg % 2]
            ready = []
            for half in range(2):
                bank = turn_banks[half]
                view = bank.buf[:, :].bitcast(F16)
                n = 0
                for k in range(2 * DC):
                    for j in range(2):
                        t = do(turned, partial(nc.tensor.transpose, view[:, n * P:(n + 1) * P], s.buf[:, 2 * half + j, k * P:(k + 1) * P], ident16[:, :]),
                            gathered[fg], bank.freed)
                        n += 1
                c = do(turned_out, cast(d.buf[:, :, half * 2 * P:(half + 1) * 2 * P], view.rearrange("p (k c) -> p k c", k=2 * DC)),
                    t, d.freed)
                bank.free(c)
                ready.append(c)
            s.free(t)
            turned_x[fg] = ready

        h_free = [[], []]
        oraw_by_name, h_f32_by_name = list(oraw), list(h_f32)

        def experts(side):
            h_free[0] = h_free[1] = [weighted_token()]
            side.until(lambda: "ids" in route_done and 0 in w_ready and not att[0].busy)
            att[0].busy = True
            for i in range(2):
                xg[i].freed = att[0].freed
                xgT[i].freed = kv_used[0]
                ysum[i].freed = kv_used[0]
                yout[i].freed = q_used[BG - 1]
                h_f32[i].freed = oraw_by_name[i].freed
            gather(0)
            gather(1)
            turn_gathered(0)
            hid = {}

            def second_layer(fg):
                ex, q = divmod(fg, NQ)
                i, hb = ex % 2, fg % 2
                ys = yout[fg % 2]
                for j in range(GT):
                    bank = acc_banks[0][j % 2]
                    cols = slice(j * P, (j + 1) * P)
                    for f in range(FC):
                        do(expert_out, mm(bank.buf[:, :], h_hi[hb][:, f, cols], w2_hl[i][:, f, :], f == 0, False,
                            skip_group_check=True), hid[fg], bank.freed)
                        t = do(expert_out, mm(bank.buf[:, 0:D], h_lo[hb][:, f, cols], w2_hl[i][:, f, 0:D], False, f == FC - 1,
                            skip_group_check=True))
                    tmp = ysum[j % 2]
                    a = do(expert_sum, partial(nc.vector.tensor_tensor, tmp.buf[:, :], bank.buf[:, D:2 * D], b2_rows[i].buf[:, :], ALU.add), t, tmp.freed)
                    a = do(expert_sum, partial(nc.vector.tensor_tensor, ys.buf[:, j, :], bank.buf[:, 0:D], tmp.buf[:, :], ALU.add), a, ys.freed)
                    tmp.free(a)
                    bank.free(a)
                    side.advance(2)
                h_free[hb] = [t]
                st = do(ys.stage, partial(nc.sync.dma_start, expert_tiles[ex, :, q * GT:(q + 1) * GT, :], ys.buf[:, :, :]), a)
                ys.free(st)
                if q == NQ - 1:
                    w_used[ex] = [t, a]

            for fg in range(FG):
                ex, q = divmod(fg, NQ)
                i, hb = ex % 2, fg % 2
                if q == 0:
                    side.until(lambda: ex in w_ready)
                xt = xgT[fg % 2]
                done = []
                for f in range(FC):
                    bank = score_banks.pop(0)
                    score_banks.append(bank)
                    cols = slice(f * P, (f + 1) * P)
                    n = 0
                    for c in range(DC):
                        for w, k in ((w1_hi, c), (w1_hi, DC + c), (w1_lo, c)):
                            t = do(hidden, mm(bank.buf[:, :], w[i][:, c, cols], xt.buf[:, k, :], n == 0, n == 3 * DC - 1),
                                turned_x[fg], bank.freed, w_ready[ex])
                            n += 1
                    hf = h_f32.pop(0)
                    h_f32.append(hf)
                    a = do(gelued, partial(nc.scalar.activation, hf.buf[:, :], bank.buf[:, :], ACT.Gelu_apprx_tanh, bias=b1T[:, ex * FC + f:ex * FC + f + 1]),
                        t, hf.freed, have["b1T"])
                    bank.free(a)
                    a = do(gelued, cast(h_hi[hb][:, f, :], hf.buf[:, :]), a, h_free[hb])
                    a2 = do(hidden_lo, partial(nc.vector.tensor_tensor, h_lo[hb][:, f, :], hf.buf[:, :], h_hi[hb][:, f, :], ALU.subtract), a, h_free[hb])
                    hf.free(a2)
                    done = [a, a2]
                    side.advance(1)
                xt.free(t)
                hid[fg] = done
                if fg + 2 < FG:
                    gather(fg + 2)
                if fg + 1 < FG:
                    turn_gathered(fg + 1)
                if fg >= 1:
                    second_layer(fg - 1)
            second_layer(FG - 1)
            experts_recorded.append([yout[0].freed[0], yout[1].freed[0]])
            att[0].free(*xg[0].freed, *xg[1].freed)
            kv_used[0] += xgT[0].freed + xgT[1].freed + w_used[E - 1] + w_used[E - 2]
            q_used[BG - 1] += yout[0].freed + yout[1].freed
            for i in range(2):
                oraw_by_name[i].freed = h_f32_by_name[i].freed
                y_got[i].freed = w_used[E - 2] + w_used[E - 1]
                x_again[i].freed = res[i].freed = y_got[i].freed
            for s in range(NP):
                p_free[s] = h_free[0] + h_free[1]
            for s in range(NLO):
                lo_free[s] = h_free[0] + h_free[1]

        side_chains = Chains(4)
        lent = [s for s in score_banks] + [s for pair in acc_banks for s in pair]
        side_banks += lent
        side_chains.add(small_transposes(), attention_weights())
        side_chains.add(*[c(g) for g in range(BG) for c in (statistics, prepare_kv)])
        side_chains.add(prepare_q(0))
        side_chains.finish()
        for s in lent:
            side_banks.remove(s)

        side_chains.add(prepare_q(1))
        side_chains.add(*[statistics(g) for g in range(BG, NG)])
        side_chains.add(route())
        for g in range(NG):
            b, gi = divmod(g, BG)
            attention(g, side_chains, 4)
            nxt = [project_out(g)]
            if g + 2 < NG:
                if gi == BG - 3:
                    nxt = [prepare_q(g + 2)] + nxt
                elif gi == BG - 2:
                    nxt = nxt + [prepare_kv(g + 2 + i) for i in range(BG)] + [prepare_q(g + 2)]
                else:
                    nxt = [prepare_q(g + 2)] + nxt
            if g == BG - 1:
                later, nxt = nxt[:1], nxt[1:]
            side_chains.add(*nxt)
            if g == BG - 1:
                side_chains.add(*[expert_weights(e) for e in range(E)])
                experts(side_chains)
                side_chains.add(*later)
            if experts_recorded and side_chains_after:
                side_chains.add(*[combine(t, None, None) for t in side_chains_after])
                side_chains_after.clear()
        side_banks += lent
        side_chains.finish()
        stores = [t for r in res for t in r.freed]

        block = ctx.enter_context(nc.Block())

        def run(engine, name):
            seen = {}
            for needs, emit, st in queues[name]:
                for s, value in needs:
                    if seen.get(id(s), 0) < value:
                        engine.wait_ge(s.sem, value)
                        seen[id(s)] = value
                emit().then_inc(st.sem, st.by)

        @block.sync
        def _(engine):
            run(engine, "sync")
            for st, value in stores:
                engine.wait_ge(st.sem, value)

        @block.tensor
        def _(engine):
            run(engine, "tensor")

        @block.vector
        def _(engine):
            run(engine, "vector")

        @block.scalar
        def _(engine):
            run(engine, "scalar")

        @block.gpsimd
        def _(engine):
            run(engine, "gpsimd")


_INS = ["L0_attn_x", "L0_attn_norm_g", "L0_attn_Wq", "L0_attn_Wkv", "L0_attn_Wout", "L0_attn_out_norm_g",
        "L0_ffn_wr", "L0_ffn_w1", "L0_ffn_b1", "L0_ffn_w2", "L0_ffn_b2"]


def kernel(**inputs):
    import concourse.bacc as bacc
    from concourse.bass_utils import run_bass_kernel_spmd

    nc = bacc.Bacc("TRN2", target_bir_lowering=False, num_devices=1)
    arrays, args = {}, []
    for name in _INS:
        a = np.ascontiguousarray(inputs[name])
        arrays[f"in_{name}"] = a
        args.append(nc.dram_tensor(f"in_{name}", a.shape, mybir.dt.from_np(a.dtype), kind="ExternalInput").ap())
    shape = arrays["in_L0_attn_x"].shape
    args.append(nc.dram_tensor("out_0", shape, F32, kind="ExternalOutput").ap())
    build_program(nc, *args)
    r = run_bass_kernel_spmd(nc, [arrays], core_ids=[0])
    return r.results[0]["out_0"]
```

```python
from contextlib import ExitStack
from functools import partial

import numpy as np

import concourse.bass as bass
from concourse import mybir

F32 = mybir.dt.float32
F16 = mybir.dt.float16
BF16 = mybir.dt.bfloat16
I32 = mybir.dt.int32
ALU = mybir.AluOpType
ACT = mybir.ActivationFunctionType
AX = mybir.AxisListType.X

P = 128
GROUP_TILES = 4
TOP_K = 2
EPS = 1e-5
SCALE = 16.0
MIN_NORM = 1e-12
BANK_F32 = 512

FIXED_US = 0.08
COLUMN_US = {"tensor": 0.0004, "scalar": 0.00083, "vector": 0.00104, "gpsimd": 0.0025}
SHARE_US = {"tensor": 0.9, "scalar": 1.4, "vector": 1.4, "gpsimd": 2.0}
AT_ONCE = 5
AT_ONCE_BEFORE = 4
COMBINE_GAP = 0.4
SCY = 3
REST = 1
STF = 0.6


class Stage:

    def __init__(self, engine, sem, by):
        self.engine, self.sem, self.by, self.count = engine, sem, by, 0


class Slot:

    def __init__(self, buf, stage=None, rest=None):
        self.buf, self.stage, self.busy, self.freed, self.rest, self.since = buf, stage, False, [], rest, 0

    def free(self, *tokens):
        self.busy, self.freed = False, list(tokens)
        self.since = self.rest.now if self.rest else 0

    def available(self):
        return not self.busy and (self.rest is None or self.rest.hurried or self.rest.now > self.since + REST)


def take(slots, n=1):
    while sum(s.available() for s in slots) < n:
        yield False
    taken = [s for s in slots if s.available()][:n]
    for slot in taken:
        slots.remove(slot)
        slots.append(slot)
        slot.busy = True
    return taken[0] if n == 1 else taken


class Chains:

    def __init__(self, at_once, share):
        self.waiting, self.running, self.at_once = [], [], at_once
        self.share, self.left, self.now, self.hurried = share, dict(share), 0, False

    def add(self, due, chain, may_start=lambda: True, needed=None):
        self.waiting.append((due, may_start, chain, due if needed is None else needed))
        self.waiting.sort(key=lambda w: w[0])

    def start(self, hurry):
        for entry in list(self.waiting):
            if sum(hurry is None or needed <= hurry for _, _, needed in self.running) >= self.at_once:
                return
            _, may_start, chain, needed = entry
            if (hurry is None or needed <= hurry) and may_start():
                self.waiting.remove(entry)
                self.running.append((chain, self.now, needed))

    def spend(self, engine, us):
        if engine in self.left:
            self.left[engine] -= us

    def turn(self, hurry=None):
        self.now += 1
        self.hurried = hurry is not None
        for k, v in self.share.items():
            self.left[k] = min(self.left[k] + v, 2 * v)
        any_moved = False
        self.start(hurry)
        for _ in range(len(self.running)):
            self.start(hurry)
            if not self.running or (hurry is None and min(self.left.values()) < 0):
                break
            chain, at, needed = self.running.pop(0)
            if (at > self.now and hurry is None) or (hurry is not None and needed > hurry):
                self.running.append((chain, at, needed))
                any_moved = any_moved or hurry is None
                continue
            moved = next(chain, "ended")
            if moved != "ended":
                self.running.append((chain, self.now + (moved or 1), needed))
            any_moved = any_moved or moved is not False
        return any_moved

    def until(self, done, group):
        while not done():
            assert self.turn(group) or self.turn(1000) or done(), "the side chains wait for each other"

    def finish(self):
        while self.waiting or self.running:
            assert self.turn(1000) or not self.running, "the side chains wait for each other"


def build_program(nc, x, norm_g, Wq, Wkv, Wout, out_norm_g, wr, w1, b1, w2, b2, out):
    B, S, D = x.shape
    INNER = Wq.shape[1]
    DH = Wkv.shape[1] // 2
    H = INNER // DH
    E, _, F = w1.shape
    T = B * S
    NT = T // P
    GT = GROUP_TILES
    GP = GT * P
    NG = NT // GT
    BG = S // GP
    KB = S // P
    DC = D // P
    FC = F // P
    IC = INNER // P
    CAP = max(8, int(max(1, T * TOP_K // E) * 1.25))
    CT = CAP // P
    ROWS = E * CAP
    VW = 2 * DH + 1
    XG = BG
    LENT = (XG + 1) % 2
    assert DH == 64 and D == 256 and GP == BANK_F32 and CAP % GP == 0 and NT * E == BANK_F32

    x_rows = x.rearrange("b s d -> (b s) d")
    out_rows = out.rearrange("b s d -> (b s) d")
    x_groups = x_rows.rearrange("(g j p) d -> g p j d", j=GT, p=P)
    x_tiles = x_rows.rearrange("(t p) d -> t p d", p=P)
    out_tiles = out_rows.rearrange("(t p) d -> t p d", p=P)

    xn_rows = nc.dram_tensor("xn_rows", [T, 2 * D], F16).ap()
    slot_token = nc.dram_tensor("slot_token", [ROWS + TOP_K * T, 1], I32).ap()
    expert_rows = nc.dram_tensor("expert_rows", [ROWS, D], F32).ap()
    attn_rows = nc.dram_tensor("attn_rows", [(XG + 1) * GP, D], F32).ap()
    xn_groups = xn_rows.rearrange("(g j p) d -> g p j d", j=GT, p=P)
    expert_tiles = expert_rows.rearrange("(e p j) d -> e p j d", p=P, j=CT)
    attn_tiles = attn_rows.rearrange("(t p) d -> t p d", p=P)

    queues = {"sync": [], "tensor": [], "vector": [], "scalar": [], "gpsimd": []}

    with ExitStack() as ctx:
        def sb(name, shape, dt):
            return ctx.enter_context(nc.sbuf_tensor(name, shape, dt))

        def stage(engine, name, by=1):
            return Stage(engine, ctx.enter_context(nc.semaphore(name)), by)

        side_stages = []

        def do(st, emit, *needs):
            flat = []
            for n in needs:
                flat += n if isinstance(n, list) else [n]
            queues[st.engine].append((flat, emit, st))
            st.count += st.by
            if st in side_stages:
                to = emit.args[0] if emit.args else emit.keywords["out"]
                columns = int(np.prod(to.shape[1:]))
                side_chains.spend(st.engine, FIXED_US + columns * COLUMN_US[st.engine])
            return st, st.count

        banks = [ctx.enter_context(nc.psum_tensor(f"bank{i}", [P, BANK_F32], F32)) for i in range(8)]
        score_banks = [Slot(b) for b in banks[0:3]]
        acc_banks = [[Slot(banks[3]), Slot(banks[4])], [Slot(banks[5]), Slot(banks[6])]]
        side_chains = Chains(AT_ONCE_BEFORE, SHARE_US)
        side_banks = [Slot(banks[7], rest=side_chains)]

        ident32 = sb("ident32", [P, P], F32)
        ident16 = sb("ident16", [P, P], F16)
        identb = sb("identb", [P, P], BF16)
        upto = sb("upto", [P, P], BF16)
        onesb = sb("onesb", [P, P], BF16)
        minus_half = sb("minus_half", [P, H], F32)
        token_id = sb("token_id", [P, NT], I32)
        zero_ids = sb("zero_ids", [P, ROWS // P], I32)
        g_cols = sb("g_cols", [P, DC], F32)
        wr_sb = sb("wr_sb", [E, D], F32)
        wrT = sb("wrT", [P, DC, E], F32)
        b1_sb = sb("b1_sb", [E * FC, P], F32)
        b1T = sb("b1T", [P, E * FC], F32)
        out_g = sb("out_g", [P, D], F32)
        wq_hi = sb("wq_hi", [P, DC, INNER], BF16)
        wq_lo = sb("wq_lo", [P, DC, INNER], BF16)
        wkv_hi = sb("wkv_hi", [P, DC, 2 * DH], BF16)
        wkv_lo = sb("wkv_lo", [P, DC, 2 * DH], BF16)
        wo_hl = sb("wo_hl", [P, IC, 2 * D], BF16)
        raws = [Slot(sb(f"raw{i}", [P, 1024], F32), stage("sync", f"raw_loaded{i}", 16)) for i in range(2)]

        mean1 = sb("mean1", [P, NT, 2], F32)
        rstd1 = sb("rstd1", [P, NT], F32)
        mean2 = sb("mean2", [P, NT, 2], F32)
        rstd2 = sb("rstd2", [P, NT], F32)
        logits = sb("logits", [P, NT, E], F32)
        gate = [sb(f"gate{k}", [P, NT], F32) for k in range(TOP_K)]
        scatter_to = [sb(f"scatter_to{k}", [P, NT], I32) for k in range(TOP_K)]
        gather_from = [sb(f"gather_from{k}", [P, NT], I32) for k in range(TOP_K)]
        slot_ids = sb("slot_ids", [P, E, CT], I32)

        xin = [Slot(sb(f"xin{i}", [P, GT, D], F32), stage("sync", f"x_loaded{i}", 16)) for i in range(2)]
        xhl = [Slot(sb(f"xhl{i}", [P, GT, 2, D], F16), stage("sync", f"xn_stored{i}", 16)) for i in range(2)]
        bn_raw = [Slot(sb(f"bn_raw{i}", [P, GT, 6], F32)) for i in range(2)]
        small = [Slot(sb(f"small{i}", [P, 4, H], F32)) for i in range(8)]
        wide = [Slot(sb(f"wide{i}", [P, 512], F32)) for i in range(4)]
        xT = [sb(f"xT{i}", [P, 2 * DC, S], F16) for i in range(1)]
        kT = [sb(f"kT{i}", [P, 2, S], F16) for i in range(2)]
        vhl_row = [sb(f"vhl{i}", [P, KB * VW], BF16) for i in range(2)]
        vhl = [v[:, :].rearrange("p (k w) -> p k w", k=KB) for v in vhl_row]
        khl = [Slot(sb("khl", [P, GT, 2, 2, DH], F16))]
        qhl = [Slot(sb(f"qhl{i}", [P, H, 2, DH], F16)) for i in range(2)]
        qT = [sb(f"qT{i}", [P, H, GP], F16) for i in range(2)]
        att = [Slot(sb(f"att{i}", [P, GT, H, DH], F32)) for i in range(2)]
        oraw = [Slot(sb(f"oraw{i}", [P, GT, VW], F32)) for i in range(2)]
        ohl = [Slot(sb(f"ohl{i}", [P, 2, INNER], BF16)) for i in range(1)]
        oT = [Slot(sb(f"oT{i}", [P, 2 * IC, P], BF16)) for i in range(1)]
        s_rows = [Slot(sb(f"s_rows{i}", [P, D], F32), stage("sync", f"s_moved{i}", 16)) for i in range(3)]

        NP, NLO, LAG = 4, 4, 3
        POOL_EVERY = 8
        PAIR = 2 * BANK_F32
        arena = sb("arena", [P, 32 * 1024], mybir.dt.uint8)
        p_f32 = arena[:, 0:NP * PAIR * 4].bitcast(F32).rearrange("p (n c) -> p n c", n=NP)
        p_top = arena[:, 0:NP * PAIR * 4].bitcast(BF16).rearrange("p (n c t) -> p n c t", n=NP, t=2)
        p_lo = arena[:, NP * PAIR * 4:NP * PAIR * 4 + NLO * PAIR * 2].bitcast(BF16).rearrange("p (n c) -> p n c", n=NLO)
        h_hi = [arena[:, i * 8192:(i + 1) * 8192].bitcast(BF16).rearrange("p (f c) -> p f c", f=FC) for i in (0, 1)]
        h_lo = [arena[:, i * 8192:(i + 1) * 8192].bitcast(BF16).rearrange("p (f c) -> p f c", f=FC) for i in (2, 3)]
        w1_hi = [sb(f"w1_hi{i}", [P, DC, F], BF16) for i in range(2)]
        w1_lo = [sb(f"w1_lo{i}", [P, DC, F], BF16) for i in range(2)]
        w2_hl = [sb(f"w2_hl{i}", [P, FC, 2 * D], BF16) for i in range(2)]

        def flat(buf, dt):
            names = " ".join("abcd"[:len(buf.shape) - 1])
            return buf[tuple([slice(None)] * len(buf.shape))].rearrange(f"p {names} -> p ({names})").bitcast(dt)

        def cut(row, i, shape):
            n = int(np.prod(shape))
            piece = row[:, i * n:(i + 1) * n]
            return piece if len(shape) == 1 else piece.rearrange("p (a b) -> p a b", a=shape[0])

        xg = [Slot(cut(flat(att[LENT].buf, F16), i, [GT, 2 * D]), stage("gpsimd", f"x_gathered{i}", 16)) for i in range(2)]
        xgT = [Slot(cut(flat(kT[0], F16), i, [2 * DC, GP])) for i in range(2)]
        yout = [Slot(cut(flat(att[XG % 2].buf, F32), i, [GT, D]), stage("sync", f"y_stored{i}", 16)) for i in range(2)]
        ysum = [Slot(cut(flat(vhl_row[0], F32), i, [D])) for i in range(2)]
        b2_rows = [Slot(cut(flat(vhl_row[0], F32), 2 + i, [D]), stage("sync", f"b2_loaded{i}", 16)) for i in range(2)]
        h_f32 = [Slot(cut(flat(oraw[i].buf, F32), 0, [GP])) for i in range(2)]
        y_got = [Slot(cut(flat(w1_lo[0], F32), i, [TOP_K, D]), stage("gpsimd", f"y_gathered{i}", 16)) for i in range(2)]
        x_again = [Slot(cut(flat(w1_lo[1], F32), i, [D]), stage("sync", f"x_again_loaded{i}", 16)) for i in range(2)]
        res = [Slot(cut(flat(w1_lo[1], F32), 2 + i, [D]), stage("sync", f"out_stored{i}", 16)) for i in range(2)]

        loaded = stage("sync", "params_loaded", 16)
        pool_const = stage("gpsimd", "pool_const")
        dve_const = stage("vector", "dve_const")
        weights_hi = stage("scalar", "weights_hi")
        weights_lo = stage("vector", "weights_lo")
        pe_side = stage("tensor", "pe_side")
        act_side = stage("scalar", "act_side")
        dve_side = stage("vector", "dve_side")
        pool_side = stage("gpsimd", "pool_side")
        side_stages += [pe_side, act_side, dve_side, pool_side, weights_hi, weights_lo]
        scattered = stage("gpsimd", "ids_scattered", 16)
        table_io = stage("sync", "table_io", 16)
        scored = stage("tensor", "scored")
        exped = stage("scalar", "exped")
        lowed = stage("vector", "lowed")
        lowed_pool = stage("gpsimd", "lowed_pool")
        weighted = stage("tensor", "weighted")
        acc_out = stage("scalar", "acc_out")
        turned = stage("tensor", "gathered_turned")
        turned_out = stage("scalar", "gathered_turned_out")
        hidden = stage("tensor", "hidden")
        gelued = stage("scalar", "gelued")
        hidden_lo = stage("vector", "hidden_lo")
        expert_out = stage("tensor", "expert_out")
        expert_sum = stage("vector", "expert_sum")

        def mm(o, w, m, start, stop, **kw):
            return partial(nc.tensor.matmul, o, w, m, start=start, stop=stop, **kw)

        def cast(o, i):
            return partial(nc.scalar.activation, o, i, ACT.Copy)

        t = do(pool_const, partial(nc.gpsimd.memset, ident32[:, :], 0.0))
        have_ident32 = do(pool_const, partial(nc.gpsimd.affine_select, out=ident32[:, :], in_=ident32[:, :], compare_op=ALU.not_equal, fill=1.0, base=0,
            pattern=[[-1, P]], channel_multiplier=1), t)
        t = do(pool_const, partial(nc.gpsimd.memset, upto[:, :], 1.0))
        have_upto = do(pool_const, partial(nc.gpsimd.affine_select, out=upto[:, :], in_=upto[:, :], compare_op=ALU.is_ge, fill=0.0, base=0,
            pattern=[[1, P]], channel_multiplier=-1), t)
        have_token_id = do(pool_const, partial(nc.gpsimd.iota, token_id[:, :], [[P, NT]], base=0, channel_multiplier=1))
        have_half = do(dve_const, partial(nc.vector.memset, minus_half[:, :], -0.5))
        have_ident16 = do(dve_const, partial(nc.vector.tensor_copy, ident16[:, :], ident32[:, :]), have_ident32)
        have_identb = do(dve_const, partial(nc.vector.tensor_copy, identb[:, :], ident32[:, :]), have_ident32)
        have_ones = do(dve_const, partial(nc.vector.memset, onesb[:, :], 1.0))
        have_zero_ids = do(dve_const, partial(nc.vector.memset, zero_ids[:, :], 0))

        do(loaded, partial(nc.sync.dma_start, g_cols[:, :], norm_g.rearrange("(c p) -> p c", p=P), allow_slow_non_contiguous=True))
        do(loaded, partial(nc.sync.dma_start, wr_sb[:, :], wr))
        do(loaded, partial(nc.sync.dma_start, b1_sb[:, :], b1.rearrange("e (f p) -> (e f) p", p=P)))
        have_params = do(loaded, partial(nc.sync.dma_start, out_g[:, :], out_norm_g.partition_broadcast(P)))
        table_zero = do(table_io, partial(nc.sync.dma_start, slot_token[0:ROWS, :].rearrange("(p j) o -> p (j o)", p=P), zero_ids[:, :]), have_zero_ids)

        def split_weight(src, width, parts, needs=()):
            slot = yield from take(raws)
            raw = slot.buf
            got = do(slot.stage, partial(nc.sync.dma_start, raw[:, 0:width].rearrange("p (a b) -> p a b", b=src.shape[2]), src), slot.freed)
            yield 3
            last = []
            for (a, b), hi, lo, scale in parts:
                if scale is None:
                    h = do(weights_hi, cast(hi, raw[:, a:b].rearrange(
                        "p (m n) -> p m n", n=hi.shape[-1])), got, *needs)
                    last.append(do(weights_lo, partial(nc.vector.tensor_tensor, lo, raw[:, a:b].rearrange("p (m n) -> p m n", n=hi.shape[-1]), hi, ALU.subtract), h, *needs))
                else:
                    h = do(weights_hi, partial(nc.scalar.activation, hi, raw[:, a:b], ACT.Copy, scale=scale),
                           got, have_params, *needs)
                    last.append(do(weights_lo, partial(nc.vector.scalar_tensor_tensor, out=lo, in0=raw[:, a:b], scalar=scale, in1=hi, op0=ALU.mult, op1=ALU.subtract), h, *needs))
                yield 3
            slot.free(*last)
            return last

        have = {}

        def attention_weights():
            r = yield from split_weight(
                Wkv.rearrange("(c p) n -> p c n", p=P), DC * 2 * DH,
                [((c * 2 * DH, (c + 1) * 2 * DH), wkv_hi[:, c, :], wkv_lo[:, c, :], g_cols[:, c:c + 1])
                 for c in range(DC)])
            have["wkv"] = r
            r = yield from split_weight(
                Wq.rearrange("(c p) n -> p c n", p=P), DC * INNER,
                [((c * INNER, (c + 1) * INNER), wq_hi[:, c, :], wq_lo[:, c, :], g_cols[:, c:c + 1])
                 for c in range(DC)])
            have["wq"] = r
            r = yield from split_weight(
                Wout.rearrange("(c p) n -> p c n", p=P), IC * D,
                [((0, IC * D), wo_hl[:, :, 0:D], wo_hl[:, :, D:2 * D], None)])
            have["wo"] = r

        def small_transposes():
            bank = yield from take(side_banks)
            ps = bank.buf
            for c in range(DC):
                a = do(pe_side, partial(nc.tensor.transpose, ps[:, c * E:(c + 1) * E], wr_sb[:, c * P:(c + 1) * P],
                                                           ident32[0:E, 0:E]), bank.freed, have_params, have_ident32)
            b = do(pe_side, partial(nc.tensor.transpose, ps[:, 64:64 + E * FC], b1_sb[:, :], ident32[0:E * FC, 0:E * FC]))
            yield
            c1 = do(act_side, cast(wrT[:, :, :], ps[:, 0:DC * E].rearrange("p (c n) -> p c n", c=DC)), a, b)
            c2 = do(act_side, cast(b1T[:, :], ps[:, 64:64 + E * FC]), b)
            bank.free(c2)
            have["wrT"], have["b1T"] = c1, c2
            yield

        stats_done = {}
        xn_stored = {}
        logits_done = {}

        def normalise(src, dst, mean, rstd, g, *needs):
            for j in range(GT):
                t = do(dve_side, partial(nc.vector.tensor_scalar, dst[:, j, :], src[:, j, :], mean[:, g * GT + j, 0:1], rstd[:, g * GT + j:g * GT + j + 1],
                    ALU.subtract, ALU.mult), *needs)
            return t

        def moments(src, mean, rstd, g, *needs):
            bn = yield from take(bn_raw)
            sm = yield from take(small)
            for j in range(GT):
                t = do(dve_side, partial(nc.vector.bn_stats, bn.buf[:, j, :], src[:, j, :]), bn.freed, *needs)
            for j in range(GT):
                t2 = do(dve_side, partial(nc.vector.bn_aggr, mean[:, g * GT + j, :], bn.buf[:, j, :]), t)
            bn.free(t2)
            t = do(dve_side, partial(nc.vector.tensor_scalar, sm.buf[:, 0, 0:GT], mean[:, g * GT:(g + 1) * GT, 1], EPS, None,
                                                       ALU.add), t2, sm.freed)
            yield
            t = do(pool_side, partial(nc.gpsimd.tensor_tensor, rstd[:, g * GT:(g + 1) * GT], sm.buf[:, 0, 0:GT],
                                                        minus_half[:, 0:GT], ALU.pow), t, have_half)
            sm.free(t)
            yield
            return t

        def statistics(g):
            xs = yield from take(xin)
            got = do(xs.stage, partial(nc.sync.dma_start, xs.buf[:, :, :], x_groups[g]), xs.freed)
            yield 3
            r = yield from moments(xs.buf, mean1, rstd1, g, got)
            xn = normalise(xs.buf, xs.buf, mean1, rstd1, g, r)
            yield 2
            r2 = yield from moments(xs.buf, mean2, rstd2, g, xn)
            stats_done[g] = r2
            hl = yield from take(xhl)
            hi = do(act_side, cast(hl.buf[:, :, 0, :], xs.buf[:, :, :]), xn, hl.freed)
            yield
            lo = do(dve_side, partial(nc.vector.tensor_tensor, hl.buf[:, :, 1, :], xs.buf[:, :, :], hl.buf[:, :, 0, :],
                                                        ALU.subtract), hi)
            st = do(hl.stage, partial(nc.sync.dma_start, xn_groups[g], hl.buf[:, :, :, :].rearrange(
                "p j k d -> p j (k d)")), lo)
            hl.free(st)
            xn_stored[g] = st
            yield 3
            turned_x = []
            xts = yield from take(wide, DC)
            for c, xt in enumerate(xts):
                bank = yield from take(side_banks)
                for j in range(GT):
                    t = do(pe_side, partial(nc.tensor.transpose, bank.buf[:, j * P:(j + 1) * P], xs.buf[:, j, c * P:(c + 1) * P], ident32[:, :]),
                        bank.freed, xn, have_ident32)
                yield
                t = do(act_side, cast(xt.buf[:, :], bank.buf[:, :]), t, xt.freed)
                bank.free(t)
                turned_x.append((xt, t))
                yield 2
            xs.free(lo, turned_x[-1][1], r2)
            bank = yield from take(side_banks)
            for j in range(GT):
                for c, (xt, ready) in enumerate(turned_x):
                    t = do(pe_side, mm(bank.buf[:, j * E:(j + 1) * E], xt.buf[:, j * P:(j + 1) * P], wrT[:, c, :],
                        start=(j == 0 and c == 0), stop=(c == DC - 1), skip_group_check=True),
                        bank.freed, ready, have["wrT"])
            for xt, _ in turned_x:
                xt.free(t)
            yield
            t = do(act_side, cast(logits[:, g * GT:(g + 1) * GT, :], bank.buf[:, 0:GT * E].rearrange(
                "p (j n) -> p j n", j=GT)), t)
            bank.free(t)
            logits_done[g] = t
            yield

        def work(buf, n):
            v = buf[:, :, :].rearrange("p a b -> p (a b)").bitcast(F32)
            return [v[:, i * 512:(i + 1) * 512].rearrange("p (t e) -> p t e", e=E) for i in range(n)]

        route_done = {}

        def route():
            iota_i = work(w2_hl[1], 4)[0].bitcast(I32)
            first, second, mask_f, row, keep, scan_a, scan_b, tmp = work(w2_hl[0], 4) + work(w1_hi[0], 2) + work(w1_lo[0], 2)
            prefer, base_row, key, total = work(w1_hi[1], 2) + work(w1_lo[1], 2)
            vecs = work(w2_hl[1], 4)[1].rearrange("p t e -> p (t e)")
            trash_v = work(w2_hl[1], 4)[2].rearrange("p t e -> p (t e)")
            m1, m2, r, dd, den, inv, pk, kk = [vecs[:, i * NT:(i + 1) * NT] for i in range(8)]
            trash = [trash_v[:, k * NT:(k + 1) * NT] for k in range(TOP_K)]
            mask16 = work(w2_hl[1], 4)[3].bitcast(BF16).rearrange("p t e -> p (t e)")[:, 0:NT * E]

            last = [list(logits_done.values()) + [have_half]]

            def v(emit, *needs):
                last[0] = [do(dve_side, emit, last[0], *needs)]

            def wide_of(a):
                return a.unsqueeze(2).to_broadcast([P, NT, E])

            i1 = do(pool_side, partial(nc.gpsimd.iota, iota_i, [[0, NT], [-1, E]], base=E, channel_multiplier=0), last[0])
            v(partial(nc.vector.tensor_copy, prefer, iota_i), i1)
            i2 = do(pool_side, partial(nc.gpsimd.iota, iota_i, [[0, NT], [CAP, E]], base=0, channel_multiplier=0), last[0])
            v(partial(nc.vector.tensor_copy, base_row, iota_i), i2)
            yield
            for k in range(TOP_K):
                ii = iota_i.rearrange("p t e -> p (t e)")[:, 0:NT]
                i3 = do(pool_side, partial(nc.gpsimd.iota, ii, [[P, NT]], base=ROWS + k * T, channel_multiplier=1), last[0])
                v(partial(nc.vector.tensor_copy, trash[k], ii), i3)
                yield
            for src, best, hot in ((logits[:, :, :], m1, first), (tmp, m2, second)):
                v(partial(nc.vector.tensor_reduce, best, src, AX, ALU.max))
                yield
                v(partial(nc.vector.tensor_tensor, key, src, wide_of(best), ALU.is_equal))
                yield
                v(partial(nc.vector.tensor_tensor, key, key, prefer, ALU.mult))
                yield
                v(partial(nc.vector.tensor_reduce, r, key, AX, ALU.max))
                yield
                v(partial(nc.vector.tensor_tensor, hot, key, wide_of(r), ALU.is_equal))
                yield
                if src is not tmp:
                    v(partial(nc.vector.scalar_tensor_tensor, out=tmp.rearrange("p t e -> p (t e)"), in0=first.rearrange("p t e -> p (t e)"), scalar=-3e38,
                        in1=logits[:, :, :].rearrange("p t e -> p (t e)"), op0=ALU.mult, op1=ALU.add))
                    yield
            v(partial(nc.vector.tensor_tensor, dd, m2, m1, ALU.subtract))
            yield 2
            ex = do(act_side, partial(nc.scalar.activation, pk, dd, ACT.Exp), last[0])
            last[0] = [ex]
            v(partial(nc.vector.tensor_scalar, den, pk, 1.0, None, ALU.add))
            v(partial(nc.vector.reciprocal, gate[0][:, :], den))
            v(partial(nc.vector.tensor_tensor, gate[1][:, :], gate[0][:, :], pk, ALU.mult))
            yield
            v(partial(nc.vector.tensor_tensor, mask_f, first, second, ALU.add))
            yield
            v(partial(nc.vector.tensor_copy, mask16.rearrange("p (t e) -> p t e", e=E), mask_f))
            yield 3
            bank = yield from take(side_banks)
            tot = do(pe_side, mm(bank.buf[:, :], onesb[:, :], mask16, True, True),
                     last[0], bank.freed, have_ones)
            yield
            v(partial(nc.vector.tensor_copy, total, bank.buf[:, :].rearrange("p (t e) -> p t e", e=E)), tot)
            inc = do(pe_side, mm(bank.buf[:, :], upto[:, :], mask16, True, True), last[0], have_upto)
            yield
            v(partial(nc.vector.tensor_copy, row, bank.buf[:, :].rearrange("p (t e) -> p t e", e=E)), inc)
            bank.free(*last[0])
            yield
            a, b, step = total, scan_a, 1
            while step < NT:
                v(partial(nc.vector.tensor_copy, b[:, 0:step, :], a[:, 0:step, :]))
                v(partial(nc.vector.tensor_tensor, b[:, step:NT, :], a[:, step:NT, :], a[:, 0:NT - step, :], ALU.add))
                yield
                a, b, step = b, (scan_b if a is total else a), step * 2
            v(partial(nc.vector.tensor_tensor, row, row, a, ALU.add))
            yield
            v(partial(nc.vector.tensor_tensor, row, row, total, ALU.subtract))
            yield
            v(partial(nc.vector.tensor_scalar, row, row, -1.0, None, ALU.add))
            yield
            v(partial(nc.vector.tensor_scalar, keep, row, float(CAP), None, ALU.is_lt))
            yield
            v(partial(nc.vector.tensor_tensor, row, row, base_row, ALU.add))
            yield
            for k, hot in ((0, first), (1, second)):
                v(partial(nc.vector.tensor_tensor, tmp, hot, row, ALU.mult))
                yield
                v(partial(nc.vector.tensor_reduce, pk, tmp, AX, ALU.add))
                yield
                v(partial(nc.vector.tensor_tensor, tmp, hot, keep, ALU.mult))
                yield
                v(partial(nc.vector.tensor_reduce, kk, tmp, AX, ALU.add))
                v(partial(nc.vector.tensor_tensor, gate[k][:, :], gate[k][:, :], kk, ALU.mult))
                v(partial(nc.vector.tensor_tensor, dd, pk, trash[k], ALU.subtract))
                v(partial(nc.vector.tensor_tensor, dd, dd, kk, ALU.mult))
                yield
                v(partial(nc.vector.tensor_tensor, dd, dd, trash[k], ALU.add))
                v(partial(nc.vector.tensor_copy, scatter_to[k][:, :], dd))
                v(partial(nc.vector.tensor_tensor, dd, pk, kk, ALU.mult))
                v(partial(nc.vector.tensor_copy, gather_from[k][:, :], dd))
                yield
            route_done["all"] = last[0]
            for t in range(NT):
                for k in range(TOP_K):
                    done = do(scattered, partial(nc.gpsimd.indirect_dma_start, slot_token, bass.IndirectOffsetOnAxis(scatter_to[k][:, t:t + 1], 0),
                        token_id[:, t:t + 1], None), last[0], table_zero, have_token_id)
                if t % 2 == 1:
                    yield SCY
            route_done["ids"] = do(table_io, partial(nc.sync.dma_start, slot_ids[:, :, :], slot_token[0:ROWS, :].rearrange("(e p j) o -> p e (j o)", p=P, j=CT)), done)
            yield 3

        kv_done = {}
        xT_used = {}
        kv_used = {}

        def turn(bank, dst_of, src_tiles, ident, dt, needs):
            view = bank.buf[:, :].bitcast(dt)
            for i, s in enumerate(src_tiles):
                t = do(pe_side, partial(nc.tensor.transpose, view[:, i * P:(i + 1) * P], s, ident[:, :]),
                       bank.freed, *needs)
            return t

        def prepare_kv(g):
            b, gi = divmod(g, BG)
            xs = yield from take(xin)
            got = do(xs.stage, partial(nc.sync.dma_start, xs.buf[:, :, :], x_groups[g]), xs.freed)
            yield 3
            t = normalise(xs.buf, xs.buf, mean1, rstd1, g, got, stats_done[g])
            yield
            xn2 = normalise(xs.buf, xs.buf, mean2, rstd2, g, t)
            yield 2
            hl = yield from take(xhl)
            hi = do(act_side, cast(hl.buf[:, :, 0, :], xs.buf[:, :, :]), xn2, hl.freed)
            yield
            lo = do(dve_side, partial(nc.vector.tensor_tensor, hl.buf[:, :, 1, :], xs.buf[:, :, :], hl.buf[:, :, 0, :],
                                                        ALU.subtract), hi)
            xs.free(lo)
            yield 2
            old = xT_used.get(g - BG, [])
            for half in range(2):
                bank = yield from take(side_banks)
                tiles = [hl.buf[:, 2 * half + j, k, c * P:(c + 1) * P] for k in range(2) for c in range(DC) for j in range(2)]
                t = turn(bank, None, tiles, ident16, F16, [lo, have_ident16])
                yield
                at = gi * GP + half * 2 * P
                ready = do(act_side, cast(xT[0][:, :, at:at + 2 * P], bank.buf[:, :].bitcast(F16).rearrange(
                    "p (k c) -> p k c", k=2 * DC)), t, *old)
                bank.free(ready)
                yield 2
            hl.free(t)
            kv, sq = yield from take(wide, 2)
            bank = yield from take(side_banks)
            W = 2 * DH
            for j in range(GT):
                at = gi * GP + j * P
                n = 0
                for kind, w in ((0, wkv_hi), (0, wkv_lo), (1, wkv_hi)):
                    for c in range(DC):
                        t = do(pe_side, mm(bank.buf[:, j * W:(j + 1) * W], xT[0][:, kind * DC + c, at:at + P], w[:, c, :],
                            start=(j == 0 and n == 0), stop=(n == 3 * DC - 1), skip_group_check=True),
                            ready, bank.freed, have["wkv"])
                        n += 1
            yield
            kvv = kv.buf[:, :].rearrange("p (j n) -> p j n", j=GT)
            t = do(act_side, cast(kv.buf[:, :], bank.buf[:, :]), t, kv.freed)
            bank.free(t)
            yield
            k_f, v_f = kvv[:, :, 0:DH], kvv[:, :, DH:W]
            V = vhl[b % 2][:, gi * GT:(gi + 1) * GT, :]
            do(dve_side, partial(nc.vector.memset, V[:, :, DH:DH + 1], 1.0), *kv_used.get(b - 2, []))
            vh = do(dve_side, partial(nc.vector.tensor_copy, V[:, :, 0:DH], v_f), t, *kv_used.get(b - 2, []))
            vl = do(dve_side, partial(nc.vector.tensor_tensor, V[:, :, DH + 1:VW], v_f, V[:, :, 0:DH], ALU.subtract), vh)
            yield
            sm = yield from take(small)
            sqv = sq.buf[:, 0:GT * DH].rearrange("p (j n) -> p j n", j=GT)
            t = do(dve_side, partial(nc.vector.tensor_tensor, sqv, k_f, k_f, ALU.mult), t, sq.freed)
            t = do(dve_side, partial(nc.vector.tensor_reduce, sm.buf[:, 0, 0:GT], sqv, AX, ALU.add), t, sm.freed)
            t = do(dve_side, partial(nc.vector.tensor_scalar, sm.buf[:, 1, 0:GT], sm.buf[:, 0, 0:GT], 1 / SCALE,
                                                       MIN_NORM ** 2 / SCALE, ALU.mult, ALU.max), t)
            yield
            t = do(pool_side, partial(nc.gpsimd.tensor_tensor, sm.buf[:, 2, 0:GT], sm.buf[:, 1, 0:GT], minus_half[:, 0:GT],
                                                        ALU.pow), t)
            yield 2
            t = do(dve_side, partial(nc.vector.tensor_tensor, sqv, k_f, sm.buf[:, 2, 0:GT].unsqueeze(2).to_broadcast([P, GT, DH]),
                                                       ALU.mult), t)
            kv.free(t, vl)
            sm.free(t)
            kn = yield from take(khl)
            twice = sqv.unsqueeze(2).to_broadcast([P, GT, 2, DH])
            t = do(dve_side, partial(nc.vector.tensor_copy, kn.buf[:, :, 0, :, :], twice), t, kn.freed)
            t = do(dve_side, partial(nc.vector.tensor_tensor, kn.buf[:, :, 1, :, :], twice, kn.buf[:, :, 0, :, :],
                                                       ALU.subtract), t)
            sq.free(t)
            yield 2
            bank = yield from take(side_banks)
            tiles = [kn.buf[:, j, k, :, :].rearrange("p a b -> p (a b)") for k in range(2) for j in range(GT)]
            t = turn(bank, None, tiles, ident16, F16, [t, have_ident16])
            kn.free(t)
            yield
            t = do(act_side, cast(kT[b % 2][:, :, gi * GP:(gi + 1) * GP], bank.buf[:, :].bitcast(
                F16).rearrange("p (k c) -> p k c", k=2)), t, *kv_used.get(b - 2, []))
            bank.free(t)
            kv_done[g] = [t, vl, ready]
            yield 2

        q_done = {}
        q_used = {}

        def prepare_q(g, j):
            b, gi = divmod(g, BG)
            at = gi * GP + j * P
            qf, sq = yield from take(wide, 2)
            bank = yield from take(side_banks)
            n = 0
            for kind, w in ((0, wq_hi), (0, wq_lo), (1, wq_hi)):
                for c in range(DC):
                    t = do(pe_side, mm(bank.buf[:, :], xT[0][:, kind * DC + c, at:at + P], w[:, c, :],
                        start=(n == 0), stop=(n == 3 * DC - 1)), kv_done[g], bank.freed, have["wq"])
                    n += 1
            last_read = t
            yield
            t = do(act_side, cast(qf.buf[:, :], bank.buf[:, :]), t, qf.freed)
            bank.free(t)
            yield
            sm = yield from take(small)
            qv, sqv = [a.buf[:, :].rearrange("p (h n) -> p h n", h=H) for a in (qf, sq)]
            t = do(pool_side, partial(nc.gpsimd.tensor_tensor, sq.buf[:, :], qf.buf[:, :], qf.buf[:, :], ALU.mult), t, sq.freed)
            yield 2
            t = do(dve_side, partial(nc.vector.tensor_reduce, sm.buf[:, 0, :], sqv, AX, ALU.add), t, sm.freed)
            t = do(dve_side, partial(nc.vector.tensor_scalar, sm.buf[:, 1, :], sm.buf[:, 0, :], SCALE ** 2 / (SCALE ** 3), MIN_NORM ** 2 / SCALE ** 3,
                ALU.mult, ALU.max), t)
            yield
            t = do(pool_side, partial(nc.gpsimd.tensor_tensor, sm.buf[:, 2, :], sm.buf[:, 1, :], minus_half[:, :], ALU.pow), t)
            yield 2
            t = do(dve_side, partial(nc.vector.tensor_tensor, sqv, qv, sm.buf[:, 2, :].unsqueeze(2).to_broadcast([P, H, DH]),
                                                       ALU.mult), t)
            qf.free(t)
            sm.free(t)
            yield 2
            hl = yield from take(qhl)
            t = do(act_side, cast(hl.buf[:, :, 0, :], sqv), t, hl.freed)
            yield
            t = do(dve_side, partial(nc.vector.tensor_tensor, hl.buf[:, :, 1, :], sqv, hl.buf[:, :, 0, :], ALU.subtract), t)
            sq.free(t)
            yield 2
            bank = yield from take(side_banks)
            t = turn(bank, None, [hl.buf[:, h, :, :].rearrange("p a b -> p (a b)") for h in range(H)],
                     ident16, F16, [t, have_ident16])
            hl.free(t)
            yield
            t = do(act_side, cast(qT[g % 2][:, :, j * P:(j + 1) * P], bank.buf[:, :].bitcast(
                F16).rearrange("p (h c) -> p h c", h=H)), t, q_used.get(g - 2, []))
            bank.free(t)
            yield
            q_done.setdefault(g, []).append(t)
            xT_used.setdefault(g, []).append(last_read)

        p_free = [[] for _ in range(NP)]
        lo_free = [[] for _ in range(NLO)]
        att_done = {}
        pairs_made = [0]
        acc_made = [0]

        def attention(g, side):
            b, gi = divmod(g, BG)
            side.until(lambda: len(q_done.get(g, [])) == GT and all(b * BG + i in kv_done for i in range(BG)), g)
            kt, V, q = kT[b % 2], vhl[b % 2], qT[g % 2]
            side.until(lambda: not att[g % 2].busy, g)
            att[g % 2].busy = True
            rows = att[g % 2]
            ready = q_done[g] + [t for i in range(BG) for t in kv_done[b * BG + i]]
            NPAIR = KB // 2
            pending = []
            after = []
            last_score = None

            def scores(h, pr):
                n = pairs_made[0]
                pairs_made[0] += 1
                slot = n % NP
                ex = []
                for i in range(2):
                    kb = 2 * pr + i
                    bank = score_banks.pop(0)
                    score_banks.append(bank)
                    for part in range(2):
                        t = do(scored, mm(bank.buf[:, :], kt[:, part, kb * P:(kb + 1) * P], q[:, h, :], part == 0, part == 1),
                            bank.freed, ready)
                    x_t = do(exped, partial(nc.scalar.activation, p_f32[:, slot, i * BANK_F32:(i + 1) * BANK_F32], bank.buf[:, :], ACT.Exp), t, p_free[slot])
                    bank.free(x_t)
                    ex.append(x_t)
                    if i == 0:
                        yield t
                lo_slot = n % NLO
                on_pool = n % POOL_EVERY == POOL_EVERY - 1
                low = do(lowed_pool if on_pool else lowed, partial((nc.gpsimd if on_pool else nc.vector).tensor_tensor, p_lo[:, lo_slot, :], p_f32[:, slot, :], p_top[:, slot, :, 1], ALU.subtract), ex, lo_free[lo_slot])
                pending.append((h, pr, slot, lo_slot, ex, low))
                yield t

            def weigh(item):
                h, pr, slot, lo_slot, ex, low = item
                accs = acc_banks[acc_made[0] % 2]
                for i in range(2):
                    kb = 2 * pr + i
                    for qb in range(GT):
                        bank = accs[qb // 2]
                        at = (qb % 2) * VW
                        cols = slice(i * BANK_F32 + qb * P, i * BANK_F32 + (qb + 1) * P)
                        do(weighted, mm(bank.buf[:, at:at + VW], p_top[:, slot, cols, 1], V[:, kb, :],
                            start=(kb == 0 and qb % 2 == 0), stop=False, skip_group_check=True), ex, bank.freed)
                        t = do(weighted, mm(bank.buf[:, at:at + DH + 1], p_lo[:, lo_slot, cols], V[:, kb, 0:DH + 1],
                            start=False, stop=(kb == KB - 1), skip_group_check=True), low)
                    if i == 0:
                        yield 3
                p_free[slot] = [t]
                lo_free[lo_slot] = [t]
                if pr == NPAIR - 1:
                    acc_made[0] += 1
                    o = next(s for s in oraw if not s.busy)
                    oraw.remove(o)
                    oraw.append(o)
                    o.busy = True
                    for k, bank in enumerate(accs):
                        c = do(acc_out, cast(o.buf[:, 2 * k:2 * k + 2, :], bank.buf[:, 0:2 * VW].rearrange("p (a b) -> p a b", a=2)),
                            t, o.freed)
                        bank.free(c)
                    after.append((h, o, c))
                yield 3

            def divide(h, o, copied):
                sm = next(s for s in oden if not s.busy)
                s = do(pool_side, partial(nc.gpsimd.tensor_tensor, osum.buf[:, :, :], o.buf[:, :, 0:DH], o.buf[:, :, DH + 1:VW],
                                                            ALU.add), copied, osum.freed)
                r = do(dve_side, partial(nc.vector.reciprocal, sm.buf[:, :, :], o.buf[:, :, DH:DH + 1]), copied, sm.freed)
                yield
                t = do(dve_side, partial(nc.vector.tensor_tensor, rows.buf[:, :, h, :], osum.buf[:, :, :],
                                                           sm.buf[:, :, :].to_broadcast([P, GT, DH]), ALU.mult),
                       s, r, rows.freed)
                osum.free(t)
                sm.free(t)
                o.free(t)
                att_done[g] = t
                yield 2

            fins = []
            for h in range(H):
                for pr in range(NPAIR):
                    sc = scores(h, pr)
                    last_score = next(sc)
                    w = weigh(pending.pop(0)) if len(pending) >= LAG else None
                    if w:
                        next(w)
                    last_score = next(sc)
                    if w:
                        for _ in w:
                            pass
                    for f in list(fins):
                        if next(f, "end") == "end":
                            fins.remove(f)
                    while after:
                        fins.append(divide(*after.pop(0)))
                    side.turn()
            q_used[g] = [last_score]
            while pending:
                for _ in weigh(pending.pop(0)):
                    pass
                side.turn()
            for f in fins + [divide(*a) for a in after]:
                for _ in f:
                    pass
            kv_used.setdefault(b, []).append(weighted_token())
            if gi == BG - 1:
                kv_used[b].append(last_score)

        def weighted_token():
            return weighted, weighted.count

        osum = Slot(sb("osum", [P, GT, DH], F32))
        oden = [Slot(sb("oden", [P, GT, 1], F32))]

        s_done = {}

        att_read = {}

        def project_out(g, j):
            rows = att[g % 2]
            ready = att_done[g]
            t_id = g * GT + j
            hl = yield from take(ohl)
            src = rows.buf[:, j, :, :].rearrange("p h d -> p (h d)")
            t = do(act_side, cast(hl.buf[:, 0, :], src), ready, hl.freed)
            yield
            t = do(dve_side, partial(nc.vector.tensor_tensor, hl.buf[:, 1, :], src, hl.buf[:, 0, :], ALU.subtract), t)
            att_read.setdefault(g, []).append(t)
            if len(att_read[g]) == GT:
                rows.free(*att_read[g])
            yield 2
            ot = yield from take(oT)
            s = yield from take(s_rows)
            wd = yield from take(wide)
            bank = yield from take(side_banks)
            t = turn(bank, None, [hl.buf[:, k, c * P:(c + 1) * P] for k in range(2) for c in range(IC)],
                     identb, BF16, [t, have_identb])
            hl.free(t)
            yield
            t = do(act_side, cast(ot.buf[:, :, :], bank.buf[:, :].bitcast(BF16).rearrange(
                "p (k c) -> p k c", k=2 * IC)), t, ot.freed)
            bank.free(t)
            yield 2
            bank = yield from take(side_banks)
            for c in range(IC):
                do(pe_side, mm(bank.buf[:, :], ot.buf[:, c, :], wo_hl[:, c, :], c == 0, False,
                                              skip_group_check=True), t, bank.freed, have["wo"])
            for c in range(IC):
                m = do(pe_side, mm(bank.buf[:, 0:D], ot.buf[:, IC + c, :], wo_hl[:, c, 0:D],
                                                  False, c == IC - 1, skip_group_check=True))
            ot.free(m)
            yield
            a = do(act_side, cast(wd.buf[:, :], bank.buf[:, :]), m, wd.freed)
            bank.free(a)
            yield
            t = do(dve_side, partial(nc.vector.tensor_tensor, wd.buf[:, D:2 * D], wd.buf[:, D:2 * D], wd.buf[:, 0:D], ALU.add), a)
            bn = yield from take(bn_raw)
            sm = yield from take(small)
            o = wd.buf[:, D:2 * D]
            t = do(dve_side, partial(nc.vector.bn_stats, bn.buf[:, 0, :], o), t, bn.freed)
            t = do(dve_side, partial(nc.vector.bn_aggr, sm.buf[:, 0, 0:2], bn.buf[:, 0, :]), t, sm.freed)
            bn.free(t)
            t = do(dve_side, partial(nc.vector.tensor_scalar, sm.buf[:, 1, 0:1], sm.buf[:, 0, 1:2], EPS, None, ALU.add), t)
            yield
            t = do(pool_side, partial(nc.gpsimd.tensor_tensor, sm.buf[:, 2, 0:1], sm.buf[:, 1, 0:1], minus_half[:, 0:1],
                                                        ALU.pow), t)
            yield 2
            t = do(dve_side, partial(nc.vector.tensor_scalar, wd.buf[:, 0:D], o, sm.buf[:, 0, 0:1], sm.buf[:, 2, 0:1],
                                                       ALU.subtract, ALU.mult), t)
            sm.free(t)
            yield
            t = do(pool_side, partial(nc.gpsimd.tensor_tensor, s.buf[:, :], wd.buf[:, 0:D], out_g[:, :], ALU.mult),
                   t, s.freed, have_params)
            wd.free(t)
            yield
            if experts_recorded:
                side_chains.add(g, combine(t_id, s, t))
            else:
                t = do(s.stage, partial(nc.sync.dma_start, attn_tiles[t_id], s.buf[:, :]), t)
                s.free(t)
                s_done[t_id] = t
                yield 3

        experts_recorded = []

        def combine(t_id, s, s_ready):
            if s is None:
                s = yield from take(s_rows)
                s_ready = do(s.stage, partial(nc.sync.dma_start, s.buf[:, :], attn_tiles[t_id]), s.freed, s_done[t_id])
            xa = yield from take(x_again)
            x_ready = do(xa.stage, partial(nc.sync.dma_start, xa.buf[:, :], x_tiles[t_id]), xa.freed)
            y = yield from take(y_got)
            for k in range(TOP_K):
                y_ready = do(y.stage, partial(nc.gpsimd.indirect_dma_start, y.buf[:, k, :], None, expert_rows, bass.IndirectOffsetOnAxis(gather_from[k][:, t_id:t_id + 1], 0)),
                    y.freed, experts_recorded[0], route_done["all"])
            yield 6
            r = yield from take(res)
            wd = yield from take(wide)
            f, w = wd.buf[:, 0:D], wd.buf[:, D:2 * D]
            t = do(dve_side, partial(nc.vector.tensor_scalar, f, y.buf[:, 0, :], gate[0][:, t_id:t_id + 1], None, ALU.mult),
                   y_ready, wd.freed)
            t = do(dve_side, partial(nc.vector.scalar_tensor_tensor, out=f, in0=y.buf[:, 1, :], scalar=gate[1][:, t_id:t_id + 1], in1=f, op0=ALU.mult, op1=ALU.add), t)
            y.free(t)
            yield 2
            t2 = do(act_side, partial(nc.scalar.activation, w, f, ACT.Tanh, scale=0.5), t)
            yield 2
            t = do(dve_side, partial(nc.vector.scalar_tensor_tensor, out=w, in0=w, scalar=1.0, in1=f, op0=ALU.add, op1=ALU.mult), t2)
            t = do(dve_side, partial(nc.vector.scalar_tensor_tensor, out=w, in0=w, scalar=0.5, in1=s.buf[:, :], op0=ALU.mult,
                                     op1=ALU.mult), t, s_ready)
            yield
            s.free(t)
            t = do(pool_side, partial(nc.gpsimd.tensor_tensor, r.buf[:, :], w, xa.buf[:, :], ALU.add), t, x_ready, r.freed)
            xa.free(t)
            wd.free(t)
            yield
            t = do(r.stage, partial(nc.sync.dma_start, out_tiles[t_id], r.buf[:, :]), t)
            r.free(t)
            yield 3

        w_ready = {}
        w_used = {}

        def expert_weights(ex):
            i = ex % 2
            needs = w_used.get(ex - 2, []) + route_done["all"]
            r = []
            w1_src = w1[ex].rearrange("(c p) f -> p c f", p=P)
            w2_src = w2[ex].rearrange("(f p) d -> p f d", p=P)
            for c in range(DC):
                r += yield from split_weight(w1_src[:, c:c + 1, :], F, [
                    ((0, F), w1_hi[i][:, c:c + 1, :], w1_lo[i][:, c:c + 1, :], None)], needs)
            for c in range(2):
                fs = slice(c * FC // 2, (c + 1) * FC // 2)
                r += yield from split_weight(w2_src[:, fs, :], FC // 2 * D, [
                    ((0, FC // 2 * D), w2_hl[i][:, fs, 0:D], w2_hl[i][:, fs, D:2 * D], None)], needs)
            bb = b2_rows[i]
            r.append(do(bb.stage, partial(nc.sync.dma_start, bb.buf[:, :], b2[ex].partition_broadcast(P)), needs, kv_used[0]))
            w_ready[ex] = r
            yield 3

        NQ = CT // GT
        FG = E * NQ
        gathered = {}
        turned_x = {}

        def gather(fg):
            ex, q = divmod(fg, NQ)
            s = xg[fg % 2]
            for j in range(GT):
                t = do(s.stage, partial(nc.gpsimd.indirect_dma_start, s.buf[:, j, :], None, xn_rows, bass.IndirectOffsetOnAxis(slot_ids[:, ex, q * GT + j:q * GT + j + 1], 0)),
                    s.freed, route_done["ids"], list(xn_stored.values()))
            gathered[fg] = t

        turn_banks = acc_banks[1]

        def turn_gathered(fg):
            s, d = xg[fg % 2], xgT[fg % 2]
            ready = []
            for half in range(2):
                bank = turn_banks[half]
                view = bank.buf[:, :].bitcast(F16)
                n = 0
                for k in range(2 * DC):
                    for j in range(2):
                        t = do(turned, partial(nc.tensor.transpose, view[:, n * P:(n + 1) * P], s.buf[:, 2 * half + j, k * P:(k + 1) * P], ident16[:, :]),
                            gathered[fg], bank.freed)
                        n += 1
                c = do(turned_out, cast(d.buf[:, :, half * 2 * P:(half + 1) * 2 * P], view.rearrange("p (k c) -> p k c", k=2 * DC)),
                    t, d.freed)
                bank.free(c)
                ready.append(c)
            s.free(t)
            turned_x[fg] = ready

        h_free = [[], []]
        oraw_by_name, h_f32_by_name = list(oraw), list(h_f32)

        def experts(side):
            h_free[0] = h_free[1] = [weighted_token()]
            side.until(lambda: "ids" in route_done and 0 in w_ready and not att[LENT].busy, XG + 0.1)
            att[LENT].busy = True
            for i in range(2):
                xg[i].freed = att[LENT].freed
                xgT[i].freed = kv_used[0]
                ysum[i].freed = kv_used[0]
                h_f32[i].freed = oraw_by_name[i].freed
            gather(0)
            gather(1)
            turn_gathered(0)
            hid = {}

            def second_layer(fg):
                ex, q = divmod(fg, NQ)
                i, hb = ex % 2, fg % 2
                ys = yout[fg % 2]
                for j in range(GT):
                    bank = acc_banks[0][j % 2]
                    cols = slice(j * P, (j + 1) * P)
                    for f in range(FC):
                        do(expert_out, mm(bank.buf[:, :], h_hi[hb][:, f, cols], w2_hl[i][:, f, :], f == 0, False,
                            skip_group_check=True), hid[fg], bank.freed)
                        t = do(expert_out, mm(bank.buf[:, 0:D], h_lo[hb][:, f, cols], w2_hl[i][:, f, 0:D], False, f == FC - 1,
                            skip_group_check=True))
                    tmp = ysum[j % 2]
                    a = do(expert_sum, partial(nc.vector.tensor_tensor, tmp.buf[:, :], bank.buf[:, D:2 * D], b2_rows[i].buf[:, :], ALU.add), t, tmp.freed)
                    a = do(expert_sum, partial(nc.vector.tensor_tensor, ys.buf[:, j, :], bank.buf[:, 0:D], tmp.buf[:, :], ALU.add), a, ys.freed)
                    tmp.free(a)
                    bank.free(a)
                    side.turn()
                h_free[hb] = [t]
                st = do(ys.stage, partial(nc.sync.dma_start, expert_tiles[ex, :, q * GT:(q + 1) * GT, :], ys.buf[:, :, :]), a)
                ys.free(st)
                if q == NQ - 1:
                    w_used[ex] = [t, a]

            for fg in range(FG):
                ex, q = divmod(fg, NQ)
                i, hb = ex % 2, fg % 2
                if q == 0:
                    side.until(lambda: ex in w_ready, XG)
                xt = xgT[fg % 2]
                done = []
                for f in range(FC):
                    bank = score_banks.pop(0)
                    score_banks.append(bank)
                    cols = slice(f * P, (f + 1) * P)
                    n = 0
                    for c in range(DC):
                        for w, k in ((w1_hi, c), (w1_hi, DC + c), (w1_lo, c)):
                            t = do(hidden, mm(bank.buf[:, :], w[i][:, c, cols], xt.buf[:, k, :], n == 0, n == 3 * DC - 1),
                                turned_x[fg], bank.freed, w_ready[ex])
                            n += 1
                    hf = h_f32.pop(0)
                    h_f32.append(hf)
                    a = do(gelued, partial(nc.scalar.activation, hf.buf[:, :], bank.buf[:, :], ACT.Gelu_apprx_tanh, bias=b1T[:, ex * FC + f:ex * FC + f + 1]),
                        t, hf.freed, have["b1T"])
                    bank.free(a)
                    a = do(gelued, cast(h_hi[hb][:, f, :], hf.buf[:, :]), a, h_free[hb])
                    a2 = do(hidden_lo, partial(nc.vector.tensor_tensor, h_lo[hb][:, f, :], hf.buf[:, :], h_hi[hb][:, f, :], ALU.subtract), a, h_free[hb])
                    hf.free(a2)
                    done = [a, a2]
                    side.turn()
                xt.free(t)
                hid[fg] = done
                if fg + 2 < FG:
                    gather(fg + 2)
                if fg + 1 < FG:
                    turn_gathered(fg + 1)
                if fg == 1:
                    side.until(lambda: not att[XG % 2].busy, XG + 2)
                    att[XG % 2].busy = True
                    yout[0].freed = yout[1].freed = att[XG % 2].freed
                if fg >= 1:
                    second_layer(fg - 1)
            second_layer(FG - 1)
            experts_recorded.append([yout[0].freed[0], yout[1].freed[0]])
            att[LENT].free(*xg[0].freed, *xg[1].freed)
            kv_used[0] += xgT[0].freed + xgT[1].freed + w_used[E - 1] + w_used[E - 2]
            att[XG % 2].free(*yout[0].freed, *yout[1].freed)
            for i in range(2):
                oraw_by_name[i].freed = h_f32_by_name[i].freed
                y_got[i].freed = w_used[E - 2] + w_used[E - 1]
                x_again[i].freed = res[i].freed = y_got[i].freed
            for s in range(NP):
                p_free[s] = h_free[0] + h_free[1]
            for s in range(NLO):
                lo_free[s] = h_free[0] + h_free[1]

        lent = [s for s in score_banks] + [s for pair in acc_banks for s in pair]
        side_banks += lent
        def add_statistics(g):
            side_chains.add((g - BG) / BG * STF, statistics(g), lambda: "wrT" in have)

        def add_kv(g):
            side_chains.add(g - BG + 0.7, prepare_kv(g), lambda: g in stats_done and "wkv" in have and (
                g < BG or len(xT_used.get(g - BG, [])) == GT))

        def add_q(g):
            for j in range(GT):
                side_chains.add(g - 0.5, prepare_q(g, j), lambda: g in kv_done and "wq" in have and (g < 2 or g - 2 in q_used))

        def add_weights(e):
            side_chains.add(XG - 0.5, expert_weights(e), lambda: "all" in route_done and len(kv_used.get(0, [])) > BG and (
                e < 2 or e - 2 in w_used))

        side_chains.add(-2, small_transposes())
        side_chains.add(-2, attention_weights())
        for g in range(BG):
            add_statistics(g)
            add_kv(g)
        add_q(0)
        side_chains.finish()
        for s in lent:
            side_banks.remove(s)

        side_chains.at_once = AT_ONCE
        add_q(1)
        for g in range(BG, NG):
            add_statistics(g)
        add_kv(BG)
        side_chains.add(0, route(), lambda: len(logits_done) == NG, XG + 0.1)
        for e in range(E):
            add_weights(e)
        later = []
        for g in range(NG):
            attention(g, side_chains)
            if g + 2 < NG:
                add_q(g + 2)
            if g + BG + 1 < NG:
                later.append(g + BG + 1)
            for j in range(GT):
                side_chains.add(g + 1.6, project_out(g, j), lambda: "wo" in have)
            if g == XG:
                experts(side_chains)
                for t in range((XG + 1) * GT):
                    side_chains.add(XG + 1 + t * COMBINE_GAP, combine(t, None, None), lambda t=t: t in s_done)
            if not BG - 1 <= g < XG:
                for n in later:
                    add_kv(n)
                later = []
        side_banks += lent
        spare = arena.rearrange("p (n c) -> p n c", c=2048)
        for i in range(GT - 1):
            ohl.append(Slot(spare[:, 3 * i, :].bitcast(BF16).rearrange("p (k c) -> p k c", k=2)))
            oT.append(Slot(spare[:, 3 * i + 1, :].bitcast(BF16).rearrange("p (k c) -> p k c", k=2 * IC)))
            wide.append(Slot(spare[:, 3 * i + 2, :].bitcast(F32)))
            ohl[-1].freed = oT[-1].freed = wide[-1].freed = [weighted_token()]
        side_chains.finish()
        stores = [t for r in res for t in r.freed]

        block = ctx.enter_context(nc.Block())

        def run(engine, name):
            seen = {}
            for needs, emit, st in queues[name]:
                for s, value in needs:
                    if seen.get(id(s), 0) < value:
                        engine.wait_ge(s.sem, value)
                        seen[id(s)] = value
                emit().then_inc(st.sem, st.by)

        @block.sync
        def _(engine):
            run(engine, "sync")
            for st, value in stores:
                engine.wait_ge(st.sem, value)

        @block.tensor
        def _(engine):
            run(engine, "tensor")

        @block.vector
        def _(engine):
            run(engine, "vector")

        @block.scalar
        def _(engine):
            run(engine, "scalar")

        @block.gpsimd
        def _(engine):
            run(engine, "gpsimd")


_INS = ["L0_attn_x", "L0_attn_norm_g", "L0_attn_Wq", "L0_attn_Wkv", "L0_attn_Wout", "L0_attn_out_norm_g",
        "L0_ffn_wr", "L0_ffn_w1", "L0_ffn_b1", "L0_ffn_w2", "L0_ffn_b2"]


def kernel(**inputs):
    import concourse.bacc as bacc
    from concourse.bass_utils import run_bass_kernel_spmd

    nc = bacc.Bacc("TRN2", target_bir_lowering=False, num_devices=1)
    arrays, args = {}, []
    for name in _INS:
        a = np.ascontiguousarray(inputs[name])
        arrays[f"in_{name}"] = a
        args.append(nc.dram_tensor(f"in_{name}", a.shape, mybir.dt.from_np(a.dtype), kind="ExternalInput").ap())
    shape = arrays["in_L0_attn_x"].shape
    args.append(nc.dram_tensor("out_0", shape, F32, kind="ExternalOutput").ap())
    build_program(nc, *args)
    r = run_bass_kernel_spmd(nc, [arrays], core_ids=[0])
    return r.results[0]["out_0"]
```

```python
from contextlib import ExitStack
from functools import partial

import numpy as np

import concourse.bass as bass
from concourse import mybir

F32 = mybir.dt.float32
F16 = mybir.dt.float16
BF16 = mybir.dt.bfloat16
I32 = mybir.dt.int32
ALU = mybir.AluOpType
ACT = mybir.ActivationFunctionType
AX = mybir.AxisListType.X

P = 128
GROUP_TILES = 4
TOP_K = 2
EPS = 1e-5
SCALE = 16.0
MIN_NORM = 1e-12
BANK_F32 = 512

FIXED_US = 0.08
COLUMN_US = {"tensor": 0.0004, "scalar": 0.00083, "vector": 0.00104, "gpsimd": 0.0025}
SHARE_US = {"tensor": 0.9, "scalar": 1.4, "vector": 1.4, "gpsimd": 2.0}
AT_ONCE_BEFORE = 5
AT_ONCE = 7
FOUR_STATISTICS_EVERY = 0.5
COMBINE_EVERY = 0.4
SCATTER_EVERY = 4


class Stage:

    def __init__(self, engine, sem, by):
        self.engine, self.sem, self.by, self.count = engine, sem, by, 0


class Slot:

    def __init__(self, buf, stage=None, rest=None):
        self.buf, self.stage, self.busy, self.freed, self.rest, self.since = buf, stage, False, [], rest, 0

    def free(self, *tokens):
        self.busy, self.freed = False, list(tokens)
        self.since = self.rest.now if self.rest else 0

    def available(self):
        return not self.busy and (self.rest is None or self.rest.hurried or self.rest.now > self.since)


def take(slots, n=1):
    while sum(s.available() for s in slots) < n:
        yield False
    taken = [s for s in slots if s.available()][:n]
    for slot in taken:
        slots.remove(slot)
        slots.append(slot)
        slot.busy = True
    return taken[0] if n == 1 else taken


class Chains:

    def __init__(self, at_once, share):
        self.waiting, self.running, self.at_once = [], [], at_once
        self.share, self.left, self.now, self.hurried = share, dict(share), 0, False

    def add(self, due, chain, may_start=lambda: True, needed=None):
        self.waiting.append((due, may_start, chain, due if needed is None else needed))
        self.waiting.sort(key=lambda w: w[0])

    def start(self, hurry):
        for entry in list(self.waiting):
            if sum(hurry is None or needed <= hurry for _, _, needed in self.running) >= self.at_once:
                return
            _, may_start, chain, needed = entry
            if (hurry is None or needed <= hurry) and may_start():
                self.waiting.remove(entry)
                self.running.append((chain, self.now, needed))

    def spend(self, engine, us):
        if engine in self.left:
            self.left[engine] -= us

    def turn(self, hurry=None):
        self.now += 1
        self.hurried = hurry is not None
        for k, v in self.share.items():
            self.left[k] = min(self.left[k] + v, 2 * v)
        any_moved = False
        self.start(hurry)
        for _ in range(len(self.running)):
            self.start(hurry)
            if not self.running or (hurry is None and min(self.left.values()) < 0):
                break
            chain, at, needed = self.running.pop(0)
            if (at > self.now and hurry is None) or (hurry is not None and needed > hurry):
                self.running.append((chain, at, needed))
                any_moved = any_moved or hurry is None
                continue
            moved = next(chain, "ended")
            if moved != "ended":
                self.running.append((chain, self.now + (moved or 1), needed))
            any_moved = any_moved or moved is not False
        return any_moved

    def until(self, done, group):
        while not done():
            assert self.turn(group) or self.turn(1000) or done(), "the side chains wait for each other"

    def finish(self):
        while self.waiting or self.running:
            assert self.turn(1000) or not self.running, "the side chains wait for each other"


def build_program(nc, x, norm_g, Wq, Wkv, Wout, out_norm_g, wr, w1, b1, w2, b2, out):
    B, S, D = x.shape
    INNER = Wq.shape[1]
    DH = Wkv.shape[1] // 2
    H = INNER // DH
    E, _, F = w1.shape
    T = B * S
    NT = T // P
    GT = GROUP_TILES
    GP = GT * P
    NG = NT // GT
    BG = S // GP
    KB = S // P
    DC = D // P
    FC = F // P
    IC = INNER // P
    CAP = max(8, int(max(1, T * TOP_K // E) * 1.25))
    CT = CAP // P
    ROWS = E * CAP
    VW = 2 * DH + 1
    XG = BG
    LENT = (XG + 1) % 2
    assert DH == 64 and D == 256 and GP == BANK_F32 and CAP % GP == 0 and NT * E == BANK_F32

    x_rows = x.rearrange("b s d -> (b s) d")
    out_rows = out.rearrange("b s d -> (b s) d")
    x_groups = x_rows.rearrange("(g j p) d -> g p j d", j=GT, p=P)
    x_tiles = x_rows.rearrange("(t p) d -> t p d", p=P)
    out_tiles = out_rows.rearrange("(t p) d -> t p d", p=P)

    xn_rows = nc.dram_tensor("xn_rows", [T, 2 * D], F16).ap()
    slot_token = nc.dram_tensor("slot_token", [ROWS + TOP_K * T, 1], I32).ap()
    expert_rows = nc.dram_tensor("expert_rows", [ROWS, D], F32).ap()
    attn_rows = nc.dram_tensor("attn_rows", [(XG + 1) * GP, D], F32).ap()
    xn_groups = xn_rows.rearrange("(g j p) d -> g p j d", j=GT, p=P)
    expert_tiles = expert_rows.rearrange("(e p j) d -> e p j d", p=P, j=CT)
    attn_tiles = attn_rows.rearrange("(t p) d -> t p d", p=P)

    queues = {"sync": [], "tensor": [], "vector": [], "scalar": [], "gpsimd": []}

    with ExitStack() as ctx:
        def sb(name, shape, dt):
            return ctx.enter_context(nc.sbuf_tensor(name, shape, dt))

        def stage(engine, name, by=1):
            return Stage(engine, ctx.enter_context(nc.semaphore(name)), by)

        side_stages = []

        def do(st, emit, *needs):
            flat = []
            for n in needs:
                flat += n if isinstance(n, list) else [n]
            queues[st.engine].append((flat, emit, st))
            st.count += st.by
            if st in side_stages:
                to = emit.args[0] if emit.args else emit.keywords["out"]
                columns = int(np.prod(to.shape[1:]))
                side_chains.spend(st.engine, FIXED_US + columns * COLUMN_US[st.engine])
            return st, st.count

        banks = [ctx.enter_context(nc.psum_tensor(f"bank{i}", [P, BANK_F32], F32)) for i in range(8)]
        score_banks = [Slot(b) for b in banks[0:3]]
        acc_banks = [[Slot(banks[3]), Slot(banks[4])], [Slot(banks[5]), Slot(banks[6])]]
        side_chains = Chains(AT_ONCE_BEFORE, SHARE_US)
        side_banks = [Slot(banks[7], rest=side_chains)]

        ident32 = sb("ident32", [P, P], F32)
        ident16 = sb("ident16", [P, P], F16)
        identb = sb("identb", [P, P], BF16)
        upto = sb("upto", [P, P], BF16)
        onesb = sb("onesb", [P, P], BF16)
        minus_half = sb("minus_half", [P, H], F32)
        token_id = sb("token_id", [P, NT], I32)
        zero_ids = sb("zero_ids", [P, ROWS // P], I32)
        g_cols = sb("g_cols", [P, DC], F32)
        wr_sb = sb("wr_sb", [E, D], F32)
        wrT = sb("wrT", [P, DC, E], F32)
        b1_sb = sb("b1_sb", [E * FC, P], F32)
        b1T = sb("b1T", [P, E * FC], F32)
        out_g = sb("out_g", [P, D], F32)
        wq_hi = sb("wq_hi", [P, DC, INNER], BF16)
        wq_lo = sb("wq_lo", [P, DC, INNER], BF16)
        wkv_hi = sb("wkv_hi", [P, DC, 2 * DH], BF16)
        wkv_lo = sb("wkv_lo", [P, DC, 2 * DH], BF16)
        wo_hl = sb("wo_hl", [P, IC, 2 * D], BF16)
        raws = [Slot(sb(f"raw{i}", [P, 1024], F32), stage("sync", f"raw_loaded{i}", 16)) for i in range(2)]

        mean1 = sb("mean1", [P, NT, 2], F32)
        rstd1 = sb("rstd1", [P, NT], F32)
        mean2 = sb("mean2", [P, NT, 2], F32)
        rstd2 = sb("rstd2", [P, NT], F32)
        logits = sb("logits", [P, NT, E], F32)
        gate = [sb(f"gate{k}", [P, NT], F32) for k in range(TOP_K)]
        scatter_to = [sb(f"scatter_to{k}", [P, NT], I32) for k in range(TOP_K)]
        gather_from = [sb(f"gather_from{k}", [P, NT], I32) for k in range(TOP_K)]
        slot_ids = sb("slot_ids", [P, E, CT], I32)

        xin = [Slot(sb(f"xin{i}", [P, GT, D], F32), stage("sync", f"x_loaded{i}", 16)) for i in range(2)]
        xhl = [Slot(sb(f"xhl{i}", [P, GT, 2, D], F16), stage("sync", f"xn_stored{i}", 16)) for i in range(2)]
        bn_raw = [Slot(sb(f"bn_raw{i}", [P, GT, 6], F32)) for i in range(2)]
        small = [Slot(sb(f"small{i}", [P, 4, H], F32)) for i in range(8)]
        wide = [Slot(sb(f"wide{i}", [P, 512], F32)) for i in range(4)]
        xT = [sb(f"xT{i}", [P, 2 * DC, S], F16) for i in range(1)]
        kT = [sb(f"kT{i}", [P, 2, S], F16) for i in range(2)]
        vhl_row = [sb(f"vhl{i}", [P, KB * VW], BF16) for i in range(2)]
        vhl = [v[:, :].rearrange("p (k w) -> p k w", k=KB) for v in vhl_row]
        khl = [Slot(sb("khl", [P, GT, 2, 2, DH], F16))]
        qhl = [Slot(sb(f"qhl{i}", [P, H, 2, DH], F16)) for i in range(2)]
        qT = [sb(f"qT{i}", [P, H, GP], F16) for i in range(2)]
        att = [Slot(sb(f"att{i}", [P, GT, H, DH], F32)) for i in range(2)]
        oraw = [Slot(sb(f"oraw{i}", [P, GT, VW], F32)) for i in range(2)]
        ohl = [Slot(sb(f"ohl{i}", [P, 2, INNER], BF16)) for i in range(1)]
        oT = [Slot(sb(f"oT{i}", [P, 2 * IC, P], BF16)) for i in range(1)]
        s_rows = [Slot(sb(f"s_rows{i}", [P, D], F32), stage("sync", f"s_moved{i}", 16)) for i in range(3)]

        NP, NLO, LAG = 4, 4, 3
        POOL_EVERY = 7
        PAIR = 2 * BANK_F32
        arena = sb("arena", [P, 32 * 1024], mybir.dt.uint8)
        p_f32 = arena[:, 0:NP * PAIR * 4].bitcast(F32).rearrange("p (n c) -> p n c", n=NP)
        p_top = arena[:, 0:NP * PAIR * 4].bitcast(BF16).rearrange("p (n c t) -> p n c t", n=NP, t=2)
        p_lo = arena[:, NP * PAIR * 4:NP * PAIR * 4 + NLO * PAIR * 2].bitcast(BF16).rearrange("p (n c) -> p n c", n=NLO)
        h_hi = [arena[:, i * 8192:(i + 1) * 8192].bitcast(BF16).rearrange("p (f c) -> p f c", f=FC) for i in (0,
            1)]
        h_lo = [arena[:, i * 8192:(i + 1) * 8192].bitcast(BF16).rearrange("p (f c) -> p f c", f=FC) for i in (2,
            3)]
        w1_hi = [sb(f"w1_hi{i}", [P, DC, F], BF16) for i in range(2)]
        w1_lo = [sb(f"w1_lo{i}", [P, DC, F], BF16) for i in range(2)]
        w2_hl = [sb(f"w2_hl{i}", [P, FC, 2 * D], BF16) for i in range(2)]

        def flat(buf, dt):
            names = " ".join("abcd"[:len(buf.shape) - 1])
            return buf[tuple([slice(None)] * len(buf.shape))].rearrange(f"p {names} -> p ({names})").bitcast(dt)

        def cut(row, i, shape):
            n = int(np.prod(shape))
            piece = row[:, i * n:(i + 1) * n]
            return piece if len(shape) == 1 else piece.rearrange("p (a b) -> p a b", a=shape[0])

        xg = [Slot(cut(flat(att[LENT].buf, F16), i, [GT, 2 * D]),
            stage("gpsimd", f"x_gathered{i}", 16)) for i in range(2)]
        xgT = [Slot(cut(flat(kT[0], F16), i, [2 * DC, GP])) for i in range(2)]
        yout = [Slot(cut(flat(att[XG % 2].buf, F32), i, [GT, D]),
            stage("sync", f"y_stored{i}", 16)) for i in range(2)]
        ysum = [Slot(cut(flat(vhl_row[0], F32), i, [D])) for i in range(2)]
        b2_rows = [Slot(cut(flat(vhl_row[0], F32), 2 + i, [D]),
            stage("sync", f"b2_loaded{i}", 16)) for i in range(2)]
        h_f32 = [Slot(cut(flat(oraw[i].buf, F32), 0, [GP])) for i in range(2)]
        y_got = [Slot(cut(flat(w1_lo[0], F32), i, [TOP_K, D]), stage("gpsimd", f"y_gathered{i}",
            16)) for i in range(2)]
        x_again = [Slot(cut(flat(w1_lo[1], F32), i, [D]), stage("sync", f"x_again_loaded{i}",
            16)) for i in range(2)]
        res = [Slot(cut(flat(w1_lo[1], F32), 2 + i, [D]), stage("sync", f"out_stored{i}",
            16)) for i in range(2)]

        loaded = stage("sync", "params_loaded", 16)
        pool_const = stage("gpsimd", "pool_const")
        dve_const = stage("vector", "dve_const")
        weights_hi = stage("scalar", "weights_hi")
        weights_lo = stage("vector", "weights_lo")
        pe_side = stage("tensor", "pe_side")
        act_side = stage("scalar", "act_side")
        dve_side = stage("vector", "dve_side")
        pool_side = stage("gpsimd", "pool_side")
        side_stages += [pe_side, act_side, dve_side, pool_side, weights_hi, weights_lo]
        scattered = stage("gpsimd", "ids_scattered", 16)
        table_io = stage("sync", "table_io", 16)
        scored = stage("tensor", "scored")
        exped = stage("scalar", "exped")
        lowed = stage("vector", "lowed")
        lowed_pool = stage("gpsimd", "lowed_pool")
        weighted = stage("tensor", "weighted")
        acc_out = stage("scalar", "acc_out")
        turned = stage("tensor", "gathered_turned")
        turned_out = stage("scalar", "gathered_turned_out")
        hidden = stage("tensor", "hidden")
        gelued = stage("scalar", "gelued")
        hidden_lo = stage("vector", "hidden_lo")
        expert_out = stage("tensor", "expert_out")
        expert_sum = stage("vector", "expert_sum")

        def mm(o, w, m, start, stop, **kw):
            return partial(nc.tensor.matmul, o, w, m, start=start, stop=stop, **kw)

        def cast(o, i):
            return partial(nc.scalar.activation, o, i, ACT.Copy)

        t = do(pool_const, partial(nc.gpsimd.memset, ident32[:, :], 0.0))
        have_ident32 = do(pool_const, partial(nc.gpsimd.affine_select, out=ident32[:, :], in_=ident32[:, :],
            compare_op=ALU.not_equal, fill=1.0, base=0,
            pattern=[[-1, P]], channel_multiplier=1), t)
        t = do(pool_const, partial(nc.gpsimd.memset, upto[:, :], 1.0))
        have_upto = do(pool_const, partial(nc.gpsimd.affine_select, out=upto[:, :], in_=upto[:, :],
            compare_op=ALU.is_ge, fill=0.0, base=0,
            pattern=[[1, P]], channel_multiplier=-1), t)
        have_token_id = do(pool_const, partial(nc.gpsimd.iota, token_id[:, :], [[P, NT]], base=0,
            channel_multiplier=1))
        have_half = do(dve_const, partial(nc.vector.memset, minus_half[:, :], -0.5))
        have_ident16 = do(dve_const, partial(nc.vector.tensor_copy, ident16[:, :], ident32[:, :]), have_ident32)
        have_identb = do(dve_const, partial(nc.vector.tensor_copy, identb[:, :], ident32[:, :]), have_ident32)
        have_ones = do(dve_const, partial(nc.vector.memset, onesb[:, :], 1.0))
        have_zero_ids = do(dve_const, partial(nc.vector.memset, zero_ids[:, :], 0))

        do(loaded, partial(nc.sync.dma_start, g_cols[:, :], norm_g.rearrange("(c p) -> p c", p=P),
            allow_slow_non_contiguous=True))
        do(loaded, partial(nc.sync.dma_start, wr_sb[:, :], wr))
        do(loaded, partial(nc.sync.dma_start, b1_sb[:, :], b1.rearrange("e (f p) -> (e f) p", p=P)))
        have_params = do(loaded, partial(nc.sync.dma_start, out_g[:, :], out_norm_g.partition_broadcast(P)))
        table_zero = do(table_io, partial(nc.sync.dma_start, slot_token[0:ROWS,
            :].rearrange("(p j) o -> p (j o)", p=P), zero_ids[:, :]), have_zero_ids)

        def split_weight(src, width, parts, needs=()):
            slot = yield from take(raws)
            raw = slot.buf
            got = do(slot.stage, partial(nc.sync.dma_start, raw[:, 0:width].rearrange("p (a b) -> p a b",
                b=src.shape[2]), src), slot.freed)
            yield 3
            last = []
            for (a, b), hi, lo, scale in parts:
                if scale is None:
                    h = do(weights_hi, cast(hi, raw[:, a:b].rearrange(
                        "p (m n) -> p m n", n=hi.shape[-1])), got, *needs)
                    last.append(do(weights_lo, partial(nc.vector.tensor_tensor, lo,
                        raw[:, a:b].rearrange("p (m n) -> p m n",
                        n=hi.shape[-1]), hi, ALU.subtract), h, *needs))
                else:
                    h = do(weights_hi, partial(nc.scalar.activation, hi, raw[:, a:b], ACT.Copy, scale=scale),
                           got, have_params, *needs)
                    last.append(do(weights_lo, partial(nc.vector.scalar_tensor_tensor, out=lo, in0=raw[:, a:b],
                        scalar=scale, in1=hi, op0=ALU.mult, op1=ALU.subtract), h, *needs))
                yield 3
            slot.free(*last)
            return last

        have = {}

        def attention_weights():
            r = yield from split_weight(
                Wkv.rearrange("(c p) n -> p c n", p=P), DC * 2 * DH,
                [((c * 2 * DH, (c + 1) * 2 * DH), wkv_hi[:, c, :], wkv_lo[:, c, :], g_cols[:, c:c + 1])
                 for c in range(DC)])
            have["wkv"] = r
            r = yield from split_weight(
                Wq.rearrange("(c p) n -> p c n", p=P), DC * INNER,
                [((c * INNER, (c + 1) * INNER), wq_hi[:, c, :], wq_lo[:, c, :], g_cols[:, c:c + 1])
                 for c in range(DC)])
            have["wq"] = r
            r = yield from split_weight(
                Wout.rearrange("(c p) n -> p c n", p=P), IC * D,
                [((0, IC * D), wo_hl[:, :, 0:D], wo_hl[:, :, D:2 * D], None)])
            have["wo"] = r

        def small_transposes():
            bank = yield from take(side_banks)
            ps = bank.buf
            for c in range(DC):
                a = do(pe_side, partial(nc.tensor.transpose, ps[:, c * E:(c + 1) * E],
                    wr_sb[:, c * P:(c + 1) * P], ident32[0:E, 0:E]), bank.freed, have_params, have_ident32)
            b = do(pe_side, partial(nc.tensor.transpose, ps[:, 64:64 + E * FC], b1_sb[:, :],
                ident32[0:E * FC, 0:E * FC]))
            yield
            c1 = do(act_side, cast(wrT[:, :, :], ps[:, 0:DC * E].rearrange("p (c n) -> p c n", c=DC)), a, b)
            c2 = do(act_side, cast(b1T[:, :], ps[:, 64:64 + E * FC]), b)
            bank.free(c2)
            have["wrT"], have["b1T"] = c1, c2
            yield

        stats_done = {}
        xn_stored = {}
        logits_done = {}

        def normalise(src, dst, mean, rstd, g, *needs):
            for j in range(GT):
                t = do(dve_side, partial(nc.vector.tensor_scalar, dst[:, j, :], src[:, j, :],
                    mean[:, g * GT + j, 0:1], rstd[:, g * GT + j:g * GT + j + 1],
                    ALU.subtract, ALU.mult), *needs)
            return t

        def moments(src, mean, rstd, g, *needs):
            bn = yield from take(bn_raw)
            sm = yield from take(small)
            for j in range(GT):
                t = do(dve_side, partial(nc.vector.bn_stats, bn.buf[:, j, :], src[:, j, :]), bn.freed, *needs)
            for j in range(GT):
                t2 = do(dve_side, partial(nc.vector.bn_aggr, mean[:, g * GT + j, :], bn.buf[:, j, :]), t)
            bn.free(t2)
            t = do(dve_side, partial(nc.vector.tensor_scalar, sm.buf[:, 0, 0:GT],
                mean[:, g * GT:(g + 1) * GT, 1], EPS, None, ALU.add), t2, sm.freed)
            yield
            t = do(pool_side, partial(nc.gpsimd.tensor_tensor, rstd[:, g * GT:(g + 1) * GT], sm.buf[:, 0, 0:GT],
                minus_half[:, 0:GT], ALU.pow), t, have_half)
            sm.free(t)
            yield
            return t

        def statistics(g):
            xs = yield from take(xin)
            got = do(xs.stage, partial(nc.sync.dma_start, xs.buf[:, :, :], x_groups[g]), xs.freed)
            yield 3
            r = yield from moments(xs.buf, mean1, rstd1, g, got)
            xn = normalise(xs.buf, xs.buf, mean1, rstd1, g, r)
            yield 2
            r2 = yield from moments(xs.buf, mean2, rstd2, g, xn)
            stats_done[g] = r2
            hl = yield from take(xhl)
            hi = do(act_side, cast(hl.buf[:, :, 0, :], xs.buf[:, :, :]), xn, hl.freed)
            yield
            lo = do(dve_side, partial(nc.vector.tensor_tensor, hl.buf[:, :, 1, :], xs.buf[:, :, :],
                hl.buf[:, :, 0, :], ALU.subtract), hi)
            st = do(hl.stage, partial(nc.sync.dma_start, xn_groups[g], hl.buf[:, :, :, :].rearrange(
                "p j k d -> p j (k d)")), lo)
            hl.free(st)
            xn_stored[g] = st
            yield 3
            turned_x = []
            xts = yield from take(wide, DC)
            for c, xt in enumerate(xts):
                bank = yield from take(side_banks)
                for j in range(GT):
                    t = do(pe_side, partial(nc.tensor.transpose, bank.buf[:, j * P:(j + 1) * P],
                        xs.buf[:, j, c * P:(c + 1) * P], ident32[:, :]),
                        bank.freed, xn, have_ident32)
                yield
                t = do(act_side, cast(xt.buf[:, :], bank.buf[:, :]), t, xt.freed)
                bank.free(t)
                turned_x.append((xt, t))
                yield 2
            xs.free(lo, turned_x[-1][1], r2)
            bank = yield from take(side_banks)
            for j in range(GT):
                for c, (xt, ready) in enumerate(turned_x):
                    t = do(pe_side, mm(bank.buf[:, j * E:(j + 1) * E], xt.buf[:, j * P:(j + 1) * P],
                        wrT[:, c, :],
                        start=(j == 0 and c == 0), stop=(c == DC - 1), skip_group_check=True),
                        bank.freed, ready, have["wrT"])
            for xt, _ in turned_x:
                xt.free(t)
            yield
            t = do(act_side, cast(logits[:, g * GT:(g + 1) * GT, :], bank.buf[:, 0:GT * E].rearrange(
                "p (j n) -> p j n", j=GT)), t)
            bank.free(t)
            logits_done[g] = t
            yield

        def work(buf, n):
            v = buf[:, :, :].rearrange("p a b -> p (a b)").bitcast(F32)
            return [v[:, i * 512:(i + 1) * 512].rearrange("p (t e) -> p t e", e=E) for i in range(n)]

        route_done = {}

        def route():
            iota_i = work(w2_hl[1], 4)[0].bitcast(I32)
            first, second, mask_f, row, keep, scan_a, scan_b, tmp = work(w2_hl[0], 4) + work(w1_hi[0],
                2) + work(w1_lo[0], 2)
            prefer, base_row, key, total = work(w1_hi[1], 2) + work(w1_lo[1], 2)
            vecs = work(w2_hl[1], 4)[1].rearrange("p t e -> p (t e)")
            trash_v = work(w2_hl[1], 4)[2].rearrange("p t e -> p (t e)")
            m1, m2, r, dd, den, inv, pk, kk = [vecs[:, i * NT:(i + 1) * NT] for i in range(8)]
            trash = [trash_v[:, k * NT:(k + 1) * NT] for k in range(TOP_K)]
            mask16 = work(w2_hl[1], 4)[3].bitcast(BF16).rearrange("p t e -> p (t e)")[:, 0:NT * E]

            last = [list(logits_done.values()) + [have_half]]

            def v(emit, *needs):
                last[0] = [do(dve_side, emit, last[0], *needs)]

            def wide_of(a):
                return a.unsqueeze(2).to_broadcast([P, NT, E])

            i1 = do(pool_side, partial(nc.gpsimd.iota, iota_i, [[0, NT], [-1, E]], base=E,
                channel_multiplier=0), last[0])
            v(partial(nc.vector.tensor_copy, prefer, iota_i), i1)
            i2 = do(pool_side, partial(nc.gpsimd.iota, iota_i, [[0, NT], [CAP, E]], base=0,
                channel_multiplier=0), last[0])
            v(partial(nc.vector.tensor_copy, base_row, iota_i), i2)
            yield
            for k in range(TOP_K):
                ii = iota_i.rearrange("p t e -> p (t e)")[:, 0:NT]
                i3 = do(pool_side, partial(nc.gpsimd.iota, ii, [[P, NT]], base=ROWS + k * T,
                    channel_multiplier=1), last[0])
                v(partial(nc.vector.tensor_copy, trash[k], ii), i3)
                yield
            for src, best, hot in ((logits[:, :, :], m1, first), (tmp, m2, second)):
                v(partial(nc.vector.tensor_reduce, best, src, AX, ALU.max))
                yield
                v(partial(nc.vector.tensor_tensor, key, src, wide_of(best), ALU.is_equal))
                yield
                v(partial(nc.vector.tensor_tensor, key, key, prefer, ALU.mult))
                yield
                v(partial(nc.vector.tensor_reduce, r, key, AX, ALU.max))
                yield
                v(partial(nc.vector.tensor_tensor, hot, key, wide_of(r), ALU.is_equal))
                yield
                if src is not tmp:
                    v(partial(nc.vector.scalar_tensor_tensor, out=tmp.rearrange("p t e -> p (t e)"),
                        in0=first.rearrange("p t e -> p (t e)"), scalar=-3e38,
                        in1=logits[:, :, :].rearrange("p t e -> p (t e)"), op0=ALU.mult, op1=ALU.add))
                    yield
            v(partial(nc.vector.tensor_tensor, dd, m2, m1, ALU.subtract))
            yield 2
            ex = do(act_side, partial(nc.scalar.activation, pk, dd, ACT.Exp), last[0])
            last[0] = [ex]
            v(partial(nc.vector.tensor_scalar, den, pk, 1.0, None, ALU.add))
            v(partial(nc.vector.reciprocal, gate[0][:, :], den))
            v(partial(nc.vector.tensor_tensor, gate[1][:, :], gate[0][:, :], pk, ALU.mult))
            yield
            v(partial(nc.vector.tensor_tensor, mask_f, first, second, ALU.add))
            yield
            v(partial(nc.vector.tensor_copy, mask16.rearrange("p (t e) -> p t e", e=E), mask_f))
            yield 3
            bank = yield from take(side_banks)
            tot = do(pe_side, mm(bank.buf[:, :], onesb[:, :], mask16, True, True),
                     last[0], bank.freed, have_ones)
            yield
            v(partial(nc.vector.tensor_copy, total, bank.buf[:, :].rearrange("p (t e) -> p t e", e=E)), tot)
            inc = do(pe_side, mm(bank.buf[:, :], upto[:, :], mask16, True, True), last[0], have_upto)
            yield
            v(partial(nc.vector.tensor_copy, row, bank.buf[:, :].rearrange("p (t e) -> p t e", e=E)), inc)
            bank.free(*last[0])
            yield
            a, b, step = total, scan_a, 1
            while step < NT:
                v(partial(nc.vector.tensor_copy, b[:, 0:step, :], a[:, 0:step, :]))
                v(partial(nc.vector.tensor_tensor, b[:, step:NT, :], a[:, step:NT, :], a[:, 0:NT - step, :],
                    ALU.add))
                yield
                a, b, step = b, (scan_b if a is total else a), step * 2
            v(partial(nc.vector.tensor_tensor, row, row, a, ALU.add))
            yield
            v(partial(nc.vector.tensor_tensor, row, row, total, ALU.subtract))
            yield
            v(partial(nc.vector.tensor_scalar, row, row, -1.0, None, ALU.add))
            yield
            v(partial(nc.vector.tensor_scalar, keep, row, float(CAP), None, ALU.is_lt))
            yield
            v(partial(nc.vector.tensor_tensor, row, row, base_row, ALU.add))
            yield
            for k, hot in ((0, first), (1, second)):
                v(partial(nc.vector.tensor_tensor, tmp, hot, row, ALU.mult))
                yield
                v(partial(nc.vector.tensor_reduce, pk, tmp, AX, ALU.add))
                yield
                v(partial(nc.vector.tensor_tensor, tmp, hot, keep, ALU.mult))
                yield
                v(partial(nc.vector.tensor_reduce, kk, tmp, AX, ALU.add))
                v(partial(nc.vector.tensor_tensor, gate[k][:, :], gate[k][:, :], kk, ALU.mult))
                v(partial(nc.vector.tensor_tensor, dd, pk, trash[k], ALU.subtract))
                v(partial(nc.vector.tensor_tensor, dd, dd, kk, ALU.mult))
                yield
                v(partial(nc.vector.tensor_tensor, dd, dd, trash[k], ALU.add))
                v(partial(nc.vector.tensor_copy, scatter_to[k][:, :], dd))
                v(partial(nc.vector.tensor_tensor, dd, pk, kk, ALU.mult))
                v(partial(nc.vector.tensor_copy, gather_from[k][:, :], dd))
                yield
            route_done["all"] = last[0]
            for t in range(NT):
                for k in range(TOP_K):
                    done = do(scattered, partial(nc.gpsimd.indirect_dma_start, slot_token,
                        bass.IndirectOffsetOnAxis(scatter_to[k][:, t:t + 1], 0),
                        token_id[:, t:t + 1], None), last[0], table_zero, have_token_id)
                if t % 2 == 1:
                    yield SCATTER_EVERY
            route_done["ids"] = do(table_io, partial(nc.sync.dma_start, slot_ids[:, :, :],
                slot_token[0:ROWS, :].rearrange("(e p j) o -> p e (j o)", p=P, j=CT)), done)
            yield 3

        kv_done = {}
        xT_used = {}
        kv_used = {}

        def turn(bank, src_tiles, ident, dt, needs):
            view = bank.buf[:, :].bitcast(dt)
            for i, s in enumerate(src_tiles):
                t = do(pe_side, partial(nc.tensor.transpose, view[:, i * P:(i + 1) * P], s, ident[:, :]),
                       bank.freed, *needs)
            return t

        def prepare_kv(g):
            b, gi = divmod(g, BG)
            xs = yield from take(xin)
            got = do(xs.stage, partial(nc.sync.dma_start, xs.buf[:, :, :], x_groups[g]), xs.freed)
            yield 3
            t = normalise(xs.buf, xs.buf, mean1, rstd1, g, got, stats_done[g])
            yield
            xn2 = normalise(xs.buf, xs.buf, mean2, rstd2, g, t)
            yield 2
            hl = yield from take(xhl)
            hi = do(act_side, cast(hl.buf[:, :, 0, :], xs.buf[:, :, :]), xn2, hl.freed)
            yield
            lo = do(dve_side, partial(nc.vector.tensor_tensor, hl.buf[:, :, 1, :], xs.buf[:, :, :],
                hl.buf[:, :, 0, :], ALU.subtract), hi)
            xs.free(lo)
            yield 3
            old = xT_used.get(g - BG, [])
            for half in range(2):
                bank = yield from take(side_banks)
                tiles = [hl.buf[:, 2 * half + j, k,
                    c * P:(c + 1) * P] for k in range(2) for c in range(DC) for j in range(2)]
                t = turn(bank, tiles, ident16, F16, [lo, have_ident16])
                yield
                at = gi * GP + half * 2 * P
                ready = do(act_side, cast(xT[0][:, :, at:at + 2 * P], bank.buf[:, :].bitcast(F16).rearrange(
                    "p (k c) -> p k c", k=2 * DC)), t, *old)
                bank.free(ready)
                yield 2
            hl.free(t)
            kv, sq = yield from take(wide, 2)
            bank = yield from take(side_banks)
            W = 2 * DH
            for j in range(GT):
                at = gi * GP + j * P
                n = 0
                for kind, w in ((0, wkv_hi), (0, wkv_lo), (1, wkv_hi)):
                    for c in range(DC):
                        t = do(pe_side, mm(bank.buf[:, j * W:(j + 1) * W], xT[0][:, kind * DC + c, at:at + P],
                            w[:, c, :],
                            start=(j == 0 and n == 0), stop=(n == 3 * DC - 1), skip_group_check=True),
                            ready, bank.freed, have["wkv"])
                        n += 1
            yield
            kvv = kv.buf[:, :].rearrange("p (j n) -> p j n", j=GT)
            t = do(act_side, cast(kv.buf[:, :], bank.buf[:, :]), t, kv.freed)
            bank.free(t)
            yield
            k_f, v_f = kvv[:, :, 0:DH], kvv[:, :, DH:W]
            V = vhl[b % 2][:, gi * GT:(gi + 1) * GT, :]
            do(dve_side, partial(nc.vector.memset, V[:, :, DH:DH + 1], 1.0), *kv_used.get(b - 2, []))
            vh = do(dve_side, partial(nc.vector.tensor_copy, V[:, :, 0:DH], v_f), t, *kv_used.get(b - 2, []))
            vl = do(dve_side, partial(nc.vector.tensor_tensor, V[:, :, DH + 1:VW], v_f, V[:, :, 0:DH],
                ALU.subtract), vh)
            yield
            sm = yield from take(small)
            sqv = sq.buf[:, 0:GT * DH].rearrange("p (j n) -> p j n", j=GT)
            t = do(dve_side, partial(nc.vector.tensor_tensor, sqv, k_f, k_f, ALU.mult), t, sq.freed)
            t = do(dve_side, partial(nc.vector.tensor_reduce, sm.buf[:, 0, 0:GT], sqv, AX, ALU.add), t,
                sm.freed)
            t = do(dve_side, partial(nc.vector.tensor_scalar, sm.buf[:, 1, 0:GT], sm.buf[:, 0, 0:GT], 1 / SCALE,
                MIN_NORM ** 2 / SCALE, ALU.mult, ALU.max), t)
            yield
            t = do(pool_side, partial(nc.gpsimd.tensor_tensor, sm.buf[:, 2, 0:GT], sm.buf[:, 1, 0:GT],
                minus_half[:, 0:GT], ALU.pow), t)
            yield 2
            t = do(dve_side, partial(nc.vector.tensor_tensor, sqv, k_f,
                sm.buf[:, 2, 0:GT].unsqueeze(2).to_broadcast([P, GT, DH]), ALU.mult), t)
            kv.free(t, vl)
            sm.free(t)
            kn = yield from take(khl)
            twice = sqv.unsqueeze(2).to_broadcast([P, GT, 2, DH])
            t = do(dve_side, partial(nc.vector.tensor_copy, kn.buf[:, :, 0, :, :], twice), t, kn.freed)
            t = do(dve_side, partial(nc.vector.tensor_tensor, kn.buf[:, :, 1, :, :], twice,
                kn.buf[:, :, 0, :, :], ALU.subtract), t)
            sq.free(t)
            yield 3
            bank = yield from take(side_banks)
            tiles = [kn.buf[:, j, k, :, :].rearrange("p a b -> p (a b)") for k in range(2) for j in range(GT)]
            t = turn(bank, tiles, ident16, F16, [t, have_ident16])
            kn.free(t)
            yield
            t = do(act_side, cast(kT[b % 2][:, :, gi * GP:(gi + 1) * GP], bank.buf[:, :].bitcast(
                F16).rearrange("p (k c) -> p k c", k=2)), t, *kv_used.get(b - 2, []))
            bank.free(t)
            kv_done[g] = [t, vl, ready]
            yield 2

        q_done = {}
        q_used = {}

        def prepare_q(g, j):
            b, gi = divmod(g, BG)
            at = gi * GP + j * P
            qf, sq = yield from take(wide, 2)
            bank = yield from take(side_banks)
            n = 0
            for kind, w in ((0, wq_hi), (0, wq_lo), (1, wq_hi)):
                for c in range(DC):
                    t = do(pe_side, mm(bank.buf[:, :], xT[0][:, kind * DC + c, at:at + P], w[:, c, :],
                        start=(n == 0), stop=(n == 3 * DC - 1)), kv_done[g], bank.freed, have["wq"])
                    n += 1
            last_read = t
            yield
            t = do(act_side, cast(qf.buf[:, :], bank.buf[:, :]), t, qf.freed)
            bank.free(t)
            yield
            sm = yield from take(small)
            qv, sqv = [a.buf[:, :].rearrange("p (h n) -> p h n", h=H) for a in (qf, sq)]
            t = do(pool_side, partial(nc.gpsimd.tensor_tensor, sq.buf[:, :], qf.buf[:, :], qf.buf[:, :],
                ALU.mult), t, sq.freed)
            yield 2
            t = do(dve_side, partial(nc.vector.tensor_reduce, sm.buf[:, 0, :], sqv, AX, ALU.add), t, sm.freed)
            t = do(dve_side, partial(nc.vector.tensor_scalar, sm.buf[:, 1, :], sm.buf[:, 0, :],
                SCALE ** 2 / (SCALE ** 3), MIN_NORM ** 2 / SCALE ** 3,
                ALU.mult, ALU.max), t)
            yield
            t = do(pool_side, partial(nc.gpsimd.tensor_tensor, sm.buf[:, 2, :], sm.buf[:, 1, :],
                minus_half[:, :], ALU.pow), t)
            yield 2
            t = do(dve_side, partial(nc.vector.tensor_tensor, sqv, qv,
                sm.buf[:, 2, :].unsqueeze(2).to_broadcast([P, H, DH]), ALU.mult), t)
            qf.free(t)
            sm.free(t)
            yield 2
            hl = yield from take(qhl)
            t = do(act_side, cast(hl.buf[:, :, 0, :], sqv), t, hl.freed)
            yield
            t = do(dve_side, partial(nc.vector.tensor_tensor, hl.buf[:, :, 1, :], sqv, hl.buf[:, :, 0, :],
                ALU.subtract), t)
            sq.free(t)
            yield 2
            bank = yield from take(side_banks)
            t = turn(bank, [hl.buf[:, h, :, :].rearrange("p a b -> p (a b)") for h in range(H)],
                     ident16, F16, [t, have_ident16])
            hl.free(t)
            yield
            t = do(act_side, cast(qT[g % 2][:, :, j * P:(j + 1) * P], bank.buf[:, :].bitcast(
                F16).rearrange("p (h c) -> p h c", h=H)), t, q_used.get(g - 2, []))
            bank.free(t)
            yield
            q_done.setdefault(g, []).append(t)
            xT_used.setdefault(g, []).append(last_read)

        p_free = [[] for _ in range(NP)]
        lo_free = [[] for _ in range(NLO)]
        att_done = {}
        pairs_made = [0]
        acc_made = [0]

        def attention(g, side):
            b, gi = divmod(g, BG)
            side.until(lambda: len(q_done.get(g, [])) == GT and all(b * BG + i in kv_done for i in range(BG)),
                g)
            kt, V, q = kT[b % 2], vhl[b % 2], qT[g % 2]
            side.until(lambda: not att[g % 2].busy, g)
            att[g % 2].busy = True
            rows = att[g % 2]
            ready = q_done[g] + [t for i in range(BG) for t in kv_done[b * BG + i]]
            NPAIR = KB // 2
            pending = []
            after = []
            last_score = None

            def scores(h, pr):
                n = pairs_made[0]
                pairs_made[0] += 1
                slot = n % NP
                ex = []
                for i in range(2):
                    kb = 2 * pr + i
                    bank = score_banks.pop(0)
                    score_banks.append(bank)
                    for part in range(2):
                        t = do(scored, mm(bank.buf[:, :], kt[:, part, kb * P:(kb + 1) * P], q[:, h, :],
                            part == 0, part == 1),
                            bank.freed, ready)
                    x_t = do(exped, partial(nc.scalar.activation,
                        p_f32[:, slot, i * BANK_F32:(i + 1) * BANK_F32], bank.buf[:,
                        :], ACT.Exp), t, p_free[slot])
                    bank.free(x_t)
                    ex.append(x_t)
                    if i == 0:
                        yield t
                lo_slot = n % NLO
                on_pool = n % POOL_EVERY == POOL_EVERY - 1
                low = do(lowed_pool if on_pool else lowed,
                    partial((nc.gpsimd if on_pool else nc.vector).tensor_tensor, p_lo[:, lo_slot, :],
                    p_f32[:, slot, :], p_top[:, slot, :, 1], ALU.subtract), ex, lo_free[lo_slot])
                pending.append((h, pr, slot, lo_slot, ex, low))
                yield t

            def weigh(item):
                h, pr, slot, lo_slot, ex, low = item
                accs = acc_banks[acc_made[0] % 2]
                for i in range(2):
                    kb = 2 * pr + i
                    for qb in range(GT):
                        bank = accs[qb // 2]
                        at = (qb % 2) * VW
                        cols = slice(i * BANK_F32 + qb * P, i * BANK_F32 + (qb + 1) * P)
                        do(weighted, mm(bank.buf[:, at:at + VW], p_top[:, slot, cols, 1], V[:, kb, :],
                            start=(kb == 0 and qb % 2 == 0), stop=False, skip_group_check=True), ex, bank.freed)
                        t = do(weighted, mm(bank.buf[:, at:at + DH + 1], p_lo[:, lo_slot, cols],
                            V[:, kb, 0:DH + 1],
                            start=False, stop=(kb == KB - 1), skip_group_check=True), low)
                    if i == 0:
                        yield 3
                p_free[slot] = [t]
                lo_free[lo_slot] = [t]
                if pr == NPAIR - 1:
                    acc_made[0] += 1
                    o = next(s for s in oraw if not s.busy)
                    oraw.remove(o)
                    oraw.append(o)
                    o.busy = True
                    for k, bank in enumerate(accs):
                        c = do(acc_out, cast(o.buf[:, 2 * k:2 * k + 2, :],
                            bank.buf[:, 0:2 * VW].rearrange("p (a b) -> p a b", a=2)),
                            t, o.freed)
                        bank.free(c)
                    after.append((h, o, c))
                yield 3

            def divide(h, o, copied):
                sm = next(s for s in oden if not s.busy)
                s = do(pool_side, partial(nc.gpsimd.tensor_tensor, osum.buf[:, :, :], o.buf[:, :, 0:DH],
                    o.buf[:, :, DH + 1:VW], ALU.add), copied, osum.freed)
                r = do(dve_side, partial(nc.vector.reciprocal, sm.buf[:, :, :], o.buf[:, :, DH:DH + 1]), copied,
                    sm.freed)
                yield
                t = do(dve_side, partial(nc.vector.tensor_tensor, rows.buf[:, :, h, :], osum.buf[:, :, :],
                    sm.buf[:, :, :].to_broadcast([P, GT, DH]), ALU.mult),
                       s, r, rows.freed)
                osum.free(t)
                sm.free(t)
                o.free(t)
                att_done[g] = t
                yield 2

            fins = []
            for h in range(H):
                for pr in range(NPAIR):
                    sc = scores(h, pr)
                    last_score = next(sc)
                    w = weigh(pending.pop(0)) if len(pending) >= LAG else None
                    if w:
                        next(w)
                    last_score = next(sc)
                    if w:
                        for _ in w:
                            pass
                    for f in list(fins):
                        if next(f, "end") == "end":
                            fins.remove(f)
                    while after:
                        fins.append(divide(*after.pop(0)))
                    side.turn()
            q_used[g] = [last_score]
            while pending:
                for _ in weigh(pending.pop(0)):
                    pass
                side.turn()
            for f in fins + [divide(*a) for a in after]:
                for _ in f:
                    pass
            kv_used.setdefault(b, []).append(weighted_token())
            if gi == BG - 1:
                kv_used[b].append(last_score)

        def weighted_token():
            return weighted, weighted.count

        osum = Slot(sb("osum", [P, GT, DH], F32))
        oden = [Slot(sb("oden", [P, GT, 1], F32))]

        s_done = {}

        att_read = {}

        def project_out(g, j):
            rows = att[g % 2]
            ready = att_done[g]
            t_id = g * GT + j
            hl = yield from take(ohl)
            src = rows.buf[:, j, :, :].rearrange("p h d -> p (h d)")
            t = do(act_side, cast(hl.buf[:, 0, :], src), ready, hl.freed)
            yield
            t = do(dve_side, partial(nc.vector.tensor_tensor, hl.buf[:, 1, :], src, hl.buf[:, 0, :],
                ALU.subtract), t)
            att_read.setdefault(g, []).append(t)
            if len(att_read[g]) == GT:
                rows.free(*att_read[g])
            yield 2
            ot = yield from take(oT)
            s = yield from take(s_rows)
            wd = yield from take(wide)
            bank = yield from take(side_banks)
            t = turn(bank, [hl.buf[:, k, c * P:(c + 1) * P] for k in range(2) for c in range(IC)],
                     identb, BF16, [t, have_identb])
            hl.free(t)
            yield
            t = do(act_side, cast(ot.buf[:, :, :], bank.buf[:, :].bitcast(BF16).rearrange(
                "p (k c) -> p k c", k=2 * IC)), t, ot.freed)
            bank.free(t)
            yield 2
            bank = yield from take(side_banks)
            for c in range(IC):
                do(pe_side, mm(bank.buf[:, :], ot.buf[:, c, :], wo_hl[:, c, :], c == 0, False,
                    skip_group_check=True), t, bank.freed, have["wo"])
            for c in range(IC):
                m = do(pe_side, mm(bank.buf[:, 0:D], ot.buf[:, IC + c, :], wo_hl[:, c, 0:D],
                False, c == IC - 1, skip_group_check=True))
            ot.free(m)
            yield
            a = do(act_side, cast(wd.buf[:, :], bank.buf[:, :]), m, wd.freed)
            bank.free(a)
            yield
            t = do(dve_side, partial(nc.vector.tensor_tensor, wd.buf[:, D:2 * D], wd.buf[:, D:2 * D],
                wd.buf[:, 0:D], ALU.add), a)
            bn = yield from take(bn_raw)
            sm = yield from take(small)
            o = wd.buf[:, D:2 * D]
            t = do(dve_side, partial(nc.vector.bn_stats, bn.buf[:, 0, :], o), t, bn.freed)
            t = do(dve_side, partial(nc.vector.bn_aggr, sm.buf[:, 0, 0:2], bn.buf[:, 0, :]), t, sm.freed)
            bn.free(t)
            t = do(dve_side, partial(nc.vector.tensor_scalar, sm.buf[:, 1, 0:1], sm.buf[:, 0, 1:2], EPS, None,
                ALU.add), t)
            yield
            t = do(pool_side, partial(nc.gpsimd.tensor_tensor, sm.buf[:, 2, 0:1], sm.buf[:, 1, 0:1],
                minus_half[:, 0:1], ALU.pow), t)
            yield 2
            t = do(dve_side, partial(nc.vector.tensor_scalar, wd.buf[:, 0:D], o, sm.buf[:, 0, 0:1],
                sm.buf[:, 2, 0:1], ALU.subtract, ALU.mult), t)
            sm.free(t)
            yield
            t = do(pool_side, partial(nc.gpsimd.tensor_tensor, s.buf[:, :], wd.buf[:, 0:D], out_g[:, :],
                ALU.mult),
                   t, s.freed, have_params)
            wd.free(t)
            yield
            if experts_recorded:
                side_chains.add(g, combine(t_id, s, t))
            else:
                t = do(s.stage, partial(nc.sync.dma_start, attn_tiles[t_id], s.buf[:, :]), t)
                s.free(t)
                s_done[t_id] = t
                yield 3

        experts_recorded = []

        def combine(t_id, s, s_ready):
            if s is None:
                s = yield from take(s_rows)
                s_ready = do(s.stage, partial(nc.sync.dma_start, s.buf[:, :], attn_tiles[t_id]), s.freed,
                    s_done[t_id])
            xa = yield from take(x_again)
            x_ready = do(xa.stage, partial(nc.sync.dma_start, xa.buf[:, :], x_tiles[t_id]), xa.freed)
            y = yield from take(y_got)
            for k in range(TOP_K):
                y_ready = do(y.stage, partial(nc.gpsimd.indirect_dma_start, y.buf[:, k, :], None, expert_rows,
                    bass.IndirectOffsetOnAxis(gather_from[k][:, t_id:t_id + 1], 0)),
                    y.freed, experts_recorded[0], route_done["all"])
            yield 6
            r = yield from take(res)
            wd = yield from take(wide)
            f, w = wd.buf[:, 0:D], wd.buf[:, D:2 * D]
            t = do(dve_side, partial(nc.vector.tensor_scalar, f, y.buf[:, 0, :], gate[0][:, t_id:t_id + 1],
                None, ALU.mult),
                   y_ready, wd.freed)
            t = do(dve_side, partial(nc.vector.scalar_tensor_tensor, out=f, in0=y.buf[:, 1, :],
                scalar=gate[1][:, t_id:t_id + 1], in1=f, op0=ALU.mult, op1=ALU.add), t)
            y.free(t)
            yield 2
            t2 = do(act_side, partial(nc.scalar.activation, w, f, ACT.Tanh, scale=0.5), t)
            yield 2
            t = do(dve_side, partial(nc.vector.scalar_tensor_tensor, out=w, in0=w, scalar=1.0, in1=f,
                op0=ALU.add, op1=ALU.mult), t2)
            t = do(dve_side, partial(nc.vector.scalar_tensor_tensor, out=w, in0=w, scalar=0.5, in1=s.buf[:, :],
                op0=ALU.mult,
                                     op1=ALU.mult), t, s_ready)
            yield
            s.free(t)
            t = do(pool_side, partial(nc.gpsimd.tensor_tensor, r.buf[:, :], w, xa.buf[:, :], ALU.add), t,
                x_ready, r.freed)
            xa.free(t)
            wd.free(t)
            yield
            t = do(r.stage, partial(nc.sync.dma_start, out_tiles[t_id], r.buf[:, :]), t)
            r.free(t)
            yield 3

        w_ready = {}
        w_used = {}

        def expert_weights(ex):
            i = ex % 2
            needs = w_used.get(ex - 2, []) + route_done["all"]
            r = []
            w1_src = w1[ex].rearrange("(c p) f -> p c f", p=P)
            w2_src = w2[ex].rearrange("(f p) d -> p f d", p=P)
            for c in range(DC):
                r += yield from split_weight(w1_src[:, c:c + 1, :], F, [
                    ((0, F), w1_hi[i][:, c:c + 1, :], w1_lo[i][:, c:c + 1, :], None)], needs)
            for c in range(2):
                fs = slice(c * FC // 2, (c + 1) * FC // 2)
                r += yield from split_weight(w2_src[:, fs, :], FC // 2 * D, [
                    ((0, FC // 2 * D), w2_hl[i][:, fs, 0:D], w2_hl[i][:, fs, D:2 * D], None)], needs)
            bb = b2_rows[i]
            r.append(do(bb.stage, partial(nc.sync.dma_start, bb.buf[:, :], b2[ex].partition_broadcast(P)),
                needs, kv_used[0]))
            w_ready[ex] = r
            yield 3

        NQ = CT // GT
        FG = E * NQ
        gathered = {}
        turned_x = {}

        def gather(fg):
            ex, q = divmod(fg, NQ)
            s = xg[fg % 2]
            for j in range(GT):
                t = do(s.stage, partial(nc.gpsimd.indirect_dma_start, s.buf[:, j, :], None, xn_rows,
                    bass.IndirectOffsetOnAxis(slot_ids[:, ex, q * GT + j:q * GT + j + 1], 0)),
                    s.freed, route_done["ids"], list(xn_stored.values()))
            gathered[fg] = t

        turn_banks = acc_banks[1]

        def turn_gathered(fg):
            s, d = xg[fg % 2], xgT[fg % 2]
            ready = []
            for half in range(2):
                bank = turn_banks[half]
                view = bank.buf[:, :].bitcast(F16)
                n = 0
                for k in range(2 * DC):
                    for j in range(2):
                        t = do(turned, partial(nc.tensor.transpose, view[:, n * P:(n + 1) * P],
                            s.buf[:, 2 * half + j, k * P:(k + 1) * P], ident16[:, :]),
                            gathered[fg], bank.freed)
                        n += 1
                c = do(turned_out, cast(d.buf[:, :, half * 2 * P:(half + 1) * 2 * P],
                    view.rearrange("p (k c) -> p k c", k=2 * DC)),
                    t, d.freed)
                bank.free(c)
                ready.append(c)
            s.free(t)
            turned_x[fg] = ready

        h_free = [[], []]
        oraw_by_name, h_f32_by_name = list(oraw), list(h_f32)

        def experts(side):
            h_free[0] = h_free[1] = [weighted_token()]
            side.until(lambda: "ids" in route_done and 0 in w_ready and not att[LENT].busy, XG + 0.1)
            att[LENT].busy = True
            for i in range(2):
                xg[i].freed = att[LENT].freed
                xgT[i].freed = kv_used[0]
                ysum[i].freed = kv_used[0]
                h_f32[i].freed = oraw_by_name[i].freed
            gather(0)
            gather(1)
            turn_gathered(0)
            hid = {}

            def second_layer(fg):
                ex, q = divmod(fg, NQ)
                i, hb = ex % 2, fg % 2
                ys = yout[fg % 2]
                for j in range(GT):
                    bank = acc_banks[0][j % 2]
                    cols = slice(j * P, (j + 1) * P)
                    for f in range(FC):
                        do(expert_out, mm(bank.buf[:, :], h_hi[hb][:, f, cols], w2_hl[i][:, f, :], f == 0,
                            False,
                            skip_group_check=True), hid[fg], bank.freed)
                        t = do(expert_out, mm(bank.buf[:, 0:D], h_lo[hb][:, f, cols], w2_hl[i][:, f, 0:D],
                            False, f == FC - 1,
                            skip_group_check=True))
                    tmp = ysum[j % 2]
                    a = do(expert_sum, partial(nc.vector.tensor_tensor, tmp.buf[:, :], bank.buf[:, D:2 * D],
                        b2_rows[i].buf[:, :], ALU.add), t, tmp.freed)
                    a = do(expert_sum, partial(nc.vector.tensor_tensor, ys.buf[:, j, :], bank.buf[:, 0:D],
                        tmp.buf[:, :], ALU.add), a, ys.freed)
                    tmp.free(a)
                    bank.free(a)
                    side.turn()
                h_free[hb] = [t]
                st = do(ys.stage, partial(nc.sync.dma_start, expert_tiles[ex, :, q * GT:(q + 1) * GT, :],
                    ys.buf[:, :, :]), a)
                ys.free(st)
                if q == NQ - 1:
                    w_used[ex] = [t, a]

            for fg in range(FG):
                ex, q = divmod(fg, NQ)
                i, hb = ex % 2, fg % 2
                if q == 0:
                    side.until(lambda: ex in w_ready, XG)
                xt = xgT[fg % 2]
                done = []
                for f in range(FC):
                    bank = score_banks.pop(0)
                    score_banks.append(bank)
                    cols = slice(f * P, (f + 1) * P)
                    n = 0
                    for c in range(DC):
                        for w, k in ((w1_hi, c), (w1_hi, DC + c), (w1_lo, c)):
                            t = do(hidden, mm(bank.buf[:, :], w[i][:, c, cols], xt.buf[:, k, :], n == 0,
                                n == 3 * DC - 1),
                                turned_x[fg], bank.freed, w_ready[ex])
                            n += 1
                    hf = h_f32.pop(0)
                    h_f32.append(hf)
                    a = do(gelued, partial(nc.scalar.activation, hf.buf[:, :], bank.buf[:, :],
                        ACT.Gelu_apprx_tanh, bias=b1T[:, ex * FC + f:ex * FC + f + 1]),
                        t, hf.freed, have["b1T"])
                    bank.free(a)
                    a = do(gelued, cast(h_hi[hb][:, f, :], hf.buf[:, :]), a, h_free[hb])
                    a2 = do(hidden_lo, partial(nc.vector.tensor_tensor, h_lo[hb][:, f, :], hf.buf[:, :],
                        h_hi[hb][:, f, :], ALU.subtract), a, h_free[hb])
                    hf.free(a2)
                    done = [a, a2]
                    side.turn()
                xt.free(t)
                hid[fg] = done
                if fg + 2 < FG:
                    gather(fg + 2)
                if fg + 1 < FG:
                    turn_gathered(fg + 1)
                if fg == 1:
                    side.until(lambda: not att[XG % 2].busy, XG + 2)
                    att[XG % 2].busy = True
                    yout[0].freed = yout[1].freed = att[XG % 2].freed
                if fg >= 1:
                    second_layer(fg - 1)
            second_layer(FG - 1)
            experts_recorded.append([yout[0].freed[0], yout[1].freed[0]])
            att[LENT].free(*xg[0].freed, *xg[1].freed)
            kv_used[0] += xgT[0].freed + xgT[1].freed + w_used[E - 1] + w_used[E - 2]
            att[XG % 2].free(*yout[0].freed, *yout[1].freed)
            for i in range(2):
                oraw_by_name[i].freed = h_f32_by_name[i].freed
                y_got[i].freed = w_used[E - 2] + w_used[E - 1]
                x_again[i].freed = res[i].freed = y_got[i].freed
            for s in range(NP):
                p_free[s] = h_free[0] + h_free[1]
            for s in range(NLO):
                lo_free[s] = h_free[0] + h_free[1]

        lent = [s for s in score_banks] + [s for pair in acc_banks for s in pair]
        side_banks += lent

        def add_statistics(g):
            side_chains.add((g - BG) / BG * FOUR_STATISTICS_EVERY, statistics(g), lambda: "wrT" in have)

        def add_kv(g):
            side_chains.add(g - BG + 0.7, prepare_kv(g), lambda: g in stats_done and "wkv" in have and (
                g < BG or len(xT_used.get(g - BG, [])) == GT))

        def add_q(g):
            for j in range(GT):
                side_chains.add(g - 0.5, prepare_q(g, j),
                    lambda: g in kv_done and "wq" in have and (g < 2 or g - 2 in q_used))

        def add_weights(e):
            side_chains.add(XG - 0.5, expert_weights(e), lambda: (
                "all" in route_done and len(kv_used.get(0, [])) > BG and (e < 2 or e - 2 in w_used)))

        side_chains.add(-2, small_transposes())
        side_chains.add(-2, attention_weights())
        for g in range(BG):
            add_statistics(g)
            add_kv(g)
        add_q(0)
        side_chains.finish()
        for s in lent:
            side_banks.remove(s)

        side_chains.at_once = AT_ONCE
        add_q(1)
        for g in range(BG, NG):
            add_statistics(g)
        add_kv(BG)
        side_chains.add(0, route(), lambda: len(logits_done) == NG, XG + 0.1)
        for e in range(E):
            add_weights(e)
        later = []
        for g in range(NG):
            attention(g, side_chains)
            if g + 2 < NG:
                add_q(g + 2)
            if g + BG + 1 < NG:
                later.append(g + BG + 1)
            for j in range(GT):
                side_chains.add(g + 1.6, project_out(g, j), lambda: "wo" in have)
            if g == XG:
                experts(side_chains)
                for t in range((XG + 1) * GT):
                    side_chains.add(XG + 1 + t * COMBINE_EVERY, combine(t, None, None), lambda t=t: t in s_done)
            if not BG - 1 <= g < XG:
                for n in later:
                    add_kv(n)
                later = []
        side_banks += lent
        spare = arena.rearrange("p (n c) -> p n c", c=2048)
        for i in range(GT - 1):
            ohl.append(Slot(spare[:, 3 * i, :].bitcast(BF16).rearrange("p (k c) -> p k c", k=2)))
            oT.append(Slot(spare[:, 3 * i + 1, :].bitcast(BF16).rearrange("p (k c) -> p k c", k=2 * IC)))
            wide.append(Slot(spare[:, 3 * i + 2, :].bitcast(F32)))
            ohl[-1].freed = oT[-1].freed = wide[-1].freed = [weighted_token()]
        side_chains.finish()
        stores = [t for r in res for t in r.freed]

        block = ctx.enter_context(nc.Block())

        def run(engine, name):
            seen = {}
            for needs, emit, st in queues[name]:
                for s, value in needs:
                    if seen.get(id(s), 0) < value:
                        engine.wait_ge(s.sem, value)
                        seen[id(s)] = value
                emit().then_inc(st.sem, st.by)

        @block.sync
        def _(engine):
            run(engine, "sync")
            for st, value in stores:
                engine.wait_ge(st.sem, value)

        @block.tensor
        def _(engine):
            run(engine, "tensor")

        @block.vector
        def _(engine):
            run(engine, "vector")

        @block.scalar
        def _(engine):
            run(engine, "scalar")

        @block.gpsimd
        def _(engine):
            run(engine, "gpsimd")


_INS = ["L0_attn_x", "L0_attn_norm_g", "L0_attn_Wq", "L0_attn_Wkv", "L0_attn_Wout", "L0_attn_out_norm_g",
        "L0_ffn_wr", "L0_ffn_w1", "L0_ffn_b1", "L0_ffn_w2", "L0_ffn_b2"]


def kernel(**inputs):
    import concourse.bacc as bacc
    from concourse.bass_utils import run_bass_kernel_spmd

    nc = bacc.Bacc("TRN2", target_bir_lowering=False, num_devices=1)
    arrays, args = {}, []
    for name in _INS:
        a = np.ascontiguousarray(inputs[name])
        arrays[f"in_{name}"] = a
        args.append(nc.dram_tensor(f"in_{name}", a.shape, mybir.dt.from_np(a.dtype), kind="ExternalInput").ap())
    shape = arrays["in_L0_attn_x"].shape
    args.append(nc.dram_tensor("out_0", shape, F32, kind="ExternalOutput").ap())
    build_program(nc, *args)
    r = run_bass_kernel_spmd(nc, [arrays], core_ids=[0])
    return r.results[0]["out_0"]
```
